# Optimizing a Trainium2 kernel written in Bass

```python
import numpy as np
import jax
import jax.numpy as jnp

def _softmax(x, axis=-1):
    return jax.nn.softmax(x, axis=axis)

def _gelu(x):
    return jax.nn.gelu(x, approximate=True)

def _silu(x):
    return jax.nn.silu(x)

def _sigmoid(x):
    return jax.nn.sigmoid(x)

def _layernorm(x, axis=-1, eps=1e-05):
    m = jnp.mean(x, axis=axis, keepdims=True)
    v = jnp.var(x, axis=axis, keepdims=True)
    return (x - m) / jnp.sqrt(v + eps)

def _scatter_add(tgt, idx, src, axis=0):
    return tgt.at[idx].add(src)

def _segment_sum(src, seg, n):
    return jax.ops.segment_sum(src, seg, n)
kernel_name = 'mk_seq_preln_d1_jaxref_r8_df53c0'

def setup_inputs(seed: int=0):
    np.random.seed(seed)
    _w = jnp.asarray

    def _L0_attn_setup():
        import jax, jax.numpy as jnp
        import numpy as np
        B, T, HID, H, DH, K = (2, 128, 128, 16, 64, 4)
        ROPE_BASE = 10000.0
        EPS = 1e-06

        def _causal_dwconv(x, w, b):
            xc = jnp.transpose(x, (0, 2, 1))
            y = jax.lax.conv_general_dilated(xc, w, window_strides=(1,), padding=[(K - 1, 0)], dimension_numbers=('NCH', 'OIH', 'NCH'), feature_group_count=xc.shape[1])
            y = y + b[None, :, None]
            return jax.nn.silu(jnp.transpose(y, (0, 2, 1)))

        def _rope(x, cos, sin):
            c = cos[None, :, None, :]
            s = sin[None, :, None, :]
            x1, x2 = (x[..., ::2], x[..., 1::2])
            return jnp.concatenate([x1 * c[..., ::2] - x2 * s[..., ::2], x1 * s[..., ::2] + x2 * c[..., ::2]], axis=-1)

        def _delta_rule(q, k, v, alpha, beta, D_param):
            qs = jnp.moveaxis(q, 1, 0).astype(jnp.float32)
            ks = jnp.moveaxis(k, 1, 0).astype(jnp.float32)
            vs = jnp.moveaxis(v, 1, 0).astype(jnp.float32)
            als = jnp.moveaxis(alpha, 1, 0).astype(jnp.float32)
            bes = jnp.moveaxis(beta, 1, 0).astype(jnp.float32)

            def step(S, inp):
                qt, kt, vt, at, bt = inp
                ot = jnp.einsum('bhd,bhde->bhe', qt, S)
                ot = ot + D_param[None, :, None] * jnp.sum(qt * kt, -1, keepdims=True) * vt
                kS = jnp.einsum('bhd,bhde->bhe', kt, S)
                at_ = at[..., None, None]
                bt_ = bt[..., None, None]
                S_new = at_ * (S - bt_ * kt[..., :, None] * kS[..., None, :]) + bt_ * kt[..., :, None] * vt[..., None, :]
                return (S_new, ot)
            S0 = jnp.zeros((q.shape[0], H, DH, DH), jnp.float32)
            _, outs = jax.lax.scan(step, S0, (qs, ks, vs, als, bes))
            return jnp.moveaxis(outs, 0, 1)

        def _forward(x, Wq, Wk, Wv, Wg, Wo, bw, bb, gkw, gkb, qcw, qcb, kcw, kcb, vcw, vcb, A_log, D_param, dt_bias, onorm_w):
            Bb, Tt, _ = x.shape
            q = _causal_dwconv(x @ Wq, qcw, qcb).reshape(Bb, Tt, H, DH)
            k = _causal_dwconv(x @ Wk, kcw, kcb).reshape(Bb, Tt, H, DH)
            v = _causal_dwconv(x @ Wv, vcw, vcb).reshape(Bb, Tt, H, DH)
            t = jnp.arange(Tt, dtype=jnp.float32)
            inv_freq = 1.0 / ROPE_BASE ** (jnp.arange(0, DH, 2, dtype=jnp.float32) / DH)
            freqs = jnp.outer(t, inv_freq)
            emb = jnp.concatenate([freqs, freqs], -1)
            cos, sin = (jnp.cos(emb), jnp.sin(emb))
            q = _rope(q, cos, sin)
            k = _rope(k, cos, sin)
            q = q * jax.lax.rsqrt(jnp.sum(q * q, -1, keepdims=True) + EPS)
            k = k * jax.lax.rsqrt(jnp.sum(k * k, -1, keepdims=True) + EPS)
            beta = jax.nn.sigmoid(x @ bw + bb)
            alpha = jnp.exp(-jnp.exp(A_log) * jax.nn.softplus(x @ gkw + gkb + dt_bias))
            o = _delta_rule(q, k, v, alpha, beta, D_param)
            g = (x @ Wg).reshape(Bb, Tt, H, DH)
            on = o * jax.lax.rsqrt(jnp.mean(o * o, -1, keepdims=True) + EPS) * onorm_w
            o = g * jax.nn.silu(on)
            return o.reshape(Bb, Tt, H * DH) @ Wo
        key = jax.random.key(seed)
        ks = jax.random.split(key, 20)
        w = lambda i, shape, s=0.02: jax.random.normal(ks[i], shape, jnp.float32) * s
        return {'x': jax.random.normal(ks[0], (B, T, HID), jnp.float32), 'Wq': w(1, (HID, H * DH)), 'Wk': w(2, (HID, H * DH)), 'Wv': w(3, (HID, H * DH)), 'Wg': w(4, (HID, H * DH)), 'Wo': w(5, (H * DH, HID)), 'bw': w(6, (HID, H)), 'bb': jnp.zeros((H,), jnp.float32), 'gkw': w(7, (HID, H)), 'gkb': jnp.zeros((H,), jnp.float32), 'qcw': w(8, (H * DH, 1, K), 0.3), 'qcb': jnp.zeros((H * DH,), jnp.float32), 'kcw': w(9, (H * DH, 1, K), 0.3), 'kcb': jnp.zeros((H * DH,), jnp.float32), 'vcw': w(10, (H * DH, 1, K), 0.3), 'vcb': jnp.zeros((H * DH,), jnp.float32), 'A_log': jnp.log(jax.random.uniform(ks[11], (H,), jnp.float32, 1.0, 16.0)), 'D_param': jnp.ones((H,), jnp.float32), 'dt_bias': jax.random.uniform(ks[12], (H,), jnp.float32, -0.01, 0.01), 'onorm_w': jnp.ones((DH,), jnp.float32)}
    _L0_attn_in = _L0_attn_setup()

    def _L0_ffn_setup():
        import jax, jax.numpy as jnp
        import numpy as np
        B, S, D, H, E, F, K = (2, 128, 128, 16, 8, 512, 2)
        EPS = 1e-05

        def _layernorm(x, g, b):
            mu = jnp.mean(x, axis=-1, keepdims=True)
            var = jnp.mean(jnp.square(x - mu), axis=-1, keepdims=True)
            return (x - mu) * jax.lax.rsqrt(var + EPS) * g + b
        key = jax.random.key(seed)
        ks = jax.random.split(key, 12)
        w = lambda k, shape: jax.random.normal(k, shape, dtype=jnp.float32) * 0.02
        return {'x': jax.random.normal(ks[0], (B, S, D), dtype=jnp.float32), 'ln1_g': jnp.ones((D,), jnp.float32), 'ln1_b': jnp.zeros((D,), jnp.float32), 'ln2_g': jnp.ones((D,), jnp.float32), 'ln2_b': jnp.zeros((D,), jnp.float32), 'Wq': w(ks[1], (D, D)), 'Wk': w(ks[2], (D, D)), 'Wv': w(ks[3], (D, D)), 'Wo': w(ks[4], (D, D)), 'Wg': w(ks[5], (D, E)), 'W1': w(ks[6], (E, D, F)), 'b1': jnp.zeros((E, F), jnp.float32), 'W2': w(ks[7], (E, F, D)), 'b2': jnp.zeros((E, D), jnp.float32)}
    _L0_ffn_in = _L0_ffn_setup()
    _d = {'L0_attn_x': _L0_attn_in['x'], 'L0_attn_Wq': _L0_attn_in['Wq'], 'L0_attn_Wk': _L0_attn_in['Wk'], 'L0_attn_Wv': _L0_attn_in['Wv'], 'L0_attn_Wg': _L0_attn_in['Wg'], 'L0_attn_Wo': _L0_attn_in['Wo'], 'L0_attn_bw': _L0_attn_in['bw'], 'L0_attn_bb': _L0_attn_in['bb'], 'L0_attn_gkw': _L0_attn_in['gkw'], 'L0_attn_gkb': _L0_attn_in['gkb'], 'L0_attn_qcw': _L0_attn_in['qcw'], 'L0_attn_qcb': _L0_attn_in['qcb'], 'L0_attn_kcw': _L0_attn_in['kcw'], 'L0_attn_kcb': _L0_attn_in['kcb'], 'L0_attn_vcw': _L0_attn_in['vcw'], 'L0_attn_vcb': _L0_attn_in['vcb'], 'L0_attn_A_log': _L0_attn_in['A_log'], 'L0_attn_D_param': _L0_attn_in['D_param'], 'L0_attn_dt_bias': _L0_attn_in['dt_bias'], 'L0_attn_onorm_w': _L0_attn_in['onorm_w'], 'L0_ffn_ln1_g': _L0_ffn_in['ln1_g'], 'L0_ffn_ln1_b': _L0_ffn_in['ln1_b'], 'L0_ffn_ln2_g': _L0_ffn_in['ln2_g'], 'L0_ffn_ln2_b': _L0_ffn_in['ln2_b'], 'L0_ffn_Wq': _L0_ffn_in['Wq'], 'L0_ffn_Wk': _L0_ffn_in['Wk'], 'L0_ffn_Wv': _L0_ffn_in['Wv'], 'L0_ffn_Wo': _L0_ffn_in['Wo'], 'L0_ffn_Wg': _L0_ffn_in['Wg'], 'L0_ffn_W1': _L0_ffn_in['W1'], 'L0_ffn_b1': _L0_ffn_in['b1'], 'L0_ffn_W2': _L0_ffn_in['W2'], 'L0_ffn_b2': _L0_ffn_in['b2']}
    _x0 = _d['L0_attn_x']
    _d['L0_attn_x'] = jax.random.normal(jax.random.fold_in(jax.random.key(seed), 1), (32, 256, 128), dtype=_x0.dtype)
    del _x0
    return _d

def reference(L0_attn_x, L0_attn_Wq, L0_attn_Wk, L0_attn_Wv, L0_attn_Wg, L0_attn_Wo, L0_attn_bw, L0_attn_bb, L0_attn_gkw, L0_attn_gkb, L0_attn_qcw, L0_attn_qcb, L0_attn_kcw, L0_attn_kcb, L0_attn_vcw, L0_attn_vcb, L0_attn_A_log, L0_attn_D_param, L0_attn_dt_bias, L0_attn_onorm_w, L0_ffn_ln1_g, L0_ffn_ln1_b, L0_ffn_ln2_g, L0_ffn_ln2_b, L0_ffn_Wq, L0_ffn_Wk, L0_ffn_Wv, L0_ffn_Wo, L0_ffn_Wg, L0_ffn_W1, L0_ffn_b1, L0_ffn_W2, L0_ffn_b2):

    def _L0_attn_ref(x, Wq, Wk, Wv, Wg, Wo, bw, bb, gkw, gkb, qcw, qcb, kcw, kcb, vcw, vcb, A_log, D_param, dt_bias, onorm_w):
        import jax, jax.numpy as jnp
        import numpy as np
        B, T, HID, H, DH, K = (2, 128, 128, 16, 64, 4)
        ROPE_BASE = 10000.0
        EPS = 1e-06

        def _causal_dwconv(x, w, b):
            xc = jnp.transpose(x, (0, 2, 1))
            y = jax.lax.conv_general_dilated(xc, w, window_strides=(1,), padding=[(K - 1, 0)], dimension_numbers=('NCH', 'OIH', 'NCH'), feature_group_count=xc.shape[1])
            y = y + b[None, :, None]
            return jax.nn.silu(jnp.transpose(y, (0, 2, 1)))

        def _rope(x, cos, sin):
            c = cos[None, :, None, :]
            s = sin[None, :, None, :]
            x1, x2 = (x[..., ::2], x[..., 1::2])
            return jnp.concatenate([x1 * c[..., ::2] - x2 * s[..., ::2], x1 * s[..., ::2] + x2 * c[..., ::2]], axis=-1)

        def _delta_rule(q, k, v, alpha, beta, D_param):
            qs = jnp.moveaxis(q, 1, 0).astype(jnp.float32)
            ks = jnp.moveaxis(k, 1, 0).astype(jnp.float32)
            vs = jnp.moveaxis(v, 1, 0).astype(jnp.float32)
            als = jnp.moveaxis(alpha, 1, 0).astype(jnp.float32)
            bes = jnp.moveaxis(beta, 1, 0).astype(jnp.float32)

            def step(S, inp):
                qt, kt, vt, at, bt = inp
                ot = jnp.einsum('bhd,bhde->bhe', qt, S)
                ot = ot + D_param[None, :, None] * jnp.sum(qt * kt, -1, keepdims=True) * vt
                kS = jnp.einsum('bhd,bhde->bhe', kt, S)
                at_ = at[..., None, None]
                bt_ = bt[..., None, None]
                S_new = at_ * (S - bt_ * kt[..., :, None] * kS[..., None, :]) + bt_ * kt[..., :, None] * vt[..., None, :]
                return (S_new, ot)
            S0 = jnp.zeros((q.shape[0], H, DH, DH), jnp.float32)
            _, outs = jax.lax.scan(step, S0, (qs, ks, vs, als, bes))
            return jnp.moveaxis(outs, 0, 1)

        def _forward(x, Wq, Wk, Wv, Wg, Wo, bw, bb, gkw, gkb, qcw, qcb, kcw, kcb, vcw, vcb, A_log, D_param, dt_bias, onorm_w):
            Bb, Tt, _ = x.shape
            q = _causal_dwconv(x @ Wq, qcw, qcb).reshape(Bb, Tt, H, DH)
            k = _causal_dwconv(x @ Wk, kcw, kcb).reshape(Bb, Tt, H, DH)
            v = _causal_dwconv(x @ Wv, vcw, vcb).reshape(Bb, Tt, H, DH)
            t = jnp.arange(Tt, dtype=jnp.float32)
            inv_freq = 1.0 / ROPE_BASE ** (jnp.arange(0, DH, 2, dtype=jnp.float32) / DH)
            freqs = jnp.outer(t, inv_freq)
            emb = jnp.concatenate([freqs, freqs], -1)
            cos, sin = (jnp.cos(emb), jnp.sin(emb))
            q = _rope(q, cos, sin)
            k = _rope(k, cos, sin)
            q = q * jax.lax.rsqrt(jnp.sum(q * q, -1, keepdims=True) + EPS)
            k = k * jax.lax.rsqrt(jnp.sum(k * k, -1, keepdims=True) + EPS)
            beta = jax.nn.sigmoid(x @ bw + bb)
            alpha = jnp.exp(-jnp.exp(A_log) * jax.nn.softplus(x @ gkw + gkb + dt_bias))
            o = _delta_rule(q, k, v, alpha, beta, D_param)
            g = (x @ Wg).reshape(Bb, Tt, H, DH)
            on = o * jax.lax.rsqrt(jnp.mean(o * o, -1, keepdims=True) + EPS) * onorm_w
            o = g * jax.nn.silu(on)
            return o.reshape(Bb, Tt, H * DH) @ Wo
        return _forward(x, Wq, Wk, Wv, Wg, Wo, bw, bb, gkw, gkb, qcw, qcb, kcw, kcb, vcw, vcb, A_log, D_param, dt_bias, onorm_w)

    def _L0_ffn_ref(x, ln1_g, ln1_b, ln2_g, ln2_b, Wq, Wk, Wv, Wo, Wg, W1, b1, W2, b2):
        import jax, jax.numpy as jnp
        import numpy as np
        B, S, D, H, E, F, K = (2, 128, 128, 16, 8, 512, 2)
        EPS = 1e-05

        def _layernorm(x, g, b):
            mu = jnp.mean(x, axis=-1, keepdims=True)
            var = jnp.mean(jnp.square(x - mu), axis=-1, keepdims=True)
            return (x - mu) * jax.lax.rsqrt(var + EPS) * g + b
        Bb, Ss, Dd = x.shape
        Dh = Dd // H
        h = _layernorm(x, ln1_g, ln1_b)
        q = (h @ Wq).reshape(Bb, Ss, H, Dh)
        k = (h @ Wk).reshape(Bb, Ss, H, Dh)
        v = (h @ Wv).reshape(Bb, Ss, H, Dh)
        scores = jnp.einsum('bqhd,bkhd->bhqk', q, k) / jnp.sqrt(jnp.float32(Dh))
        attn = jax.nn.softmax(scores, axis=-1)
        ctx = jnp.einsum('bhqk,bkhd->bqhd', attn, v).reshape(Bb, Ss, Dd)
        x = x + ctx @ Wo
        m = _layernorm(x, ln2_g, ln2_b)
        xt = m.reshape(-1, Dd)
        T = xt.shape[0]
        probs = jax.nn.softmax(xt @ Wg, axis=-1)
        wts, idx = jax.lax.top_k(probs, K)
        wts = wts / jnp.sum(wts, axis=-1, keepdims=True)
        h1 = jax.nn.gelu(jnp.einsum('td,edf->etf', xt, W1) + b1[:, None, :])
        ye = jnp.einsum('etf,efd->etd', h1, W2) + b2[:, None, :]
        sel = ye[idx, jnp.arange(T)[:, None], :]
        moe_out = jnp.sum(wts[..., None] * sel, axis=1).reshape(Bb, Ss, Dd)
        return x + moe_out
    x = L0_attn_x
    x = x + _L0_attn_ref(_layernorm(x, axis=-1), L0_attn_Wq, L0_attn_Wk, L0_attn_Wv, L0_attn_Wg, L0_attn_Wo, L0_attn_bw, L0_attn_bb, L0_attn_gkw, L0_attn_gkb, L0_attn_qcw, L0_attn_qcb, L0_attn_kcw, L0_attn_kcb, L0_attn_vcw, L0_attn_vcb, L0_attn_A_log, L0_attn_D_param, L0_attn_dt_bias, L0_attn_onorm_w)
    x = x + _L0_ffn_ref(_layernorm(x, axis=-1), L0_ffn_ln1_g, L0_ffn_ln1_b, L0_ffn_ln2_g, L0_ffn_ln2_b, L0_ffn_Wq, L0_ffn_Wk, L0_ffn_Wv, L0_ffn_Wo, L0_ffn_Wg, L0_ffn_W1, L0_ffn_b1, L0_ffn_W2, L0_ffn_b2)
    return x

_drawn_inputs = setup_inputs


def setup_inputs(seed=0):
    import zlib

    import numpy as np

    out = dict(_drawn_inputs(seed))
    spreads = {'L0_attn_bb': (0.0, 0.8),
     'L0_attn_gkb': (0.0, 2.0),
     'L0_attn_qcb': (0.0, 0.1),
     'L0_attn_kcb': (0.0, 0.1),
     'L0_attn_vcb': (0.0, 0.1),
     'L0_attn_D_param': (1.0, 0.6),
     'L0_attn_onorm_w': (1.0, 0.6),
     'L0_ffn_ln1_g': (1.0, 0.6),
     'L0_ffn_ln1_b': (0.0, 0.8),
     'L0_ffn_ln2_g': (1.0, 0.6),
     'L0_ffn_ln2_b': (0.0, 0.8),
     'L0_ffn_b1': (0.0, 0.8),
     'L0_ffn_b2': (0.0, 0.636)}
    factors = {'L0_attn_bw': 8.0,
     'L0_attn_gkw': 34.926,
     'L0_attn_A_log': 5.838,
     'L0_attn_dt_bias': 64.0,
     'L0_ffn_Wq': 8.0,
     'L0_ffn_Wk': 8.0,
     'L0_ffn_Wv': 8.0,
     'L0_ffn_Wo': 8.0,
     'L0_ffn_W1': 2.916}
    for name, (base, spread) in spreads.items():
        noise = np.random.default_rng([zlib.crc32(name.encode()), seed]).standard_normal(out[name].shape)
        drawn = base * np.exp(spread * noise) if base else spread * noise
        out[name] = jnp.asarray(drawn.astype(out[name].dtype))
    for name, factor in factors.items():
        out[name] = (out[name] * factor).astype(out[name].dtype)
    return out
```

```python
from contextlib import ExitStack

import numpy as np
import concourse.bass as bass
from concourse import mybir

F32 = mybir.dt.float32
BF16 = mybir.dt.bfloat16
ALU = mybir.AluOpType
ACT = mybir.ActivationFunctionType
AX = mybir.AxisListType

P = 128
T = 256
NT = T // P
HID = 128
H = 16
DH = 64
CH = H * DH
NC = CH // P
KT = 4
PAD = KT - 1
NU = NT * H
FH = 16
FD = HID // FH
NE = 8
FF = 512
NF = FF // P
SB = 32
GW = P + 1
EPS_NORM = 1e-6
EPS_LN = 1e-5
NCONV = 3 * NC // 2
NS = 3
ROW6 = 6 * FD
SPLIT_Q = (0, 0, 1, 0, 2, 1)
SPLIT_K = (0, 1, 0, 2, 0, 1)


class Signal:

    def __init__(self, sem, per):
        self.sem, self.per = sem, per

    def at(self, i, k):
        if isinstance(i, tuple):
            return i[0] * self.per + (k - i[1] * self.per)
        return i * self.per + k


def bank_uses():
    g = [("xT", 0, "xnT_ready", 1), ("gate", 1, "v_gate", 1)]
    g += [(("qk", c), c % 4, "v_conv", 6 * (c + 1)) for c in range(4)]
    g += [("alphaT", 1, "v_alpha", 7), ("GT", 2, "v_Gc", 1), ("sums", 4, "v_sum", 2)]
    g += [(("qk", c), c % 4, "v_conv", 6 * (c + 1)) for c in range(4, NC)]
    g += [(("v", m), m % 2, "v_conv", 6 * (NC + m + 1)) for m in range(4)]
    g += [(("vT", t, half), 2 + t, "v_V", 2 * half + t + 1) for half in range(2) for t in range(NT)]
    for h in range(H):
        g += [(("alpha", h), h % 2, "v_Gam", h + 1), (("kk", h), 2 + h % 2, "v_NP", h + 1)]
    g += [(("kT", half), half, "v_Kt", 2 + half) for half in range(2)]
    g += [(("join1", half), 2 + half, "a_T1", half + 1) for half in range(2)]
    g += [(("join2", half), half, "a_Z", 2) for half in range(2)]
    for t in range(NT):
        for half in range(2):
            g += [(("top", t, half), half, "a_W", 4 * t + half + 1),
                  (("cross", t, half), 2 + half, "v_R", 4 * t + half + 1),
                  (("low", t, half), half, "a_W", 4 * t + half + 3)]
        if not t:
            g += [("S", 4, "a_S", 1)]
            for half in range(2):
                g += [(("KS", half), 2 + half, "v_R", 3 + half), (("QS", half), 2 + half, "v_QS", half + 1)]
        g += [(("o", t, half), 2 + half, "v_O", 2 * t + half + 1) for half in range(2)]
    g += [(("g", t, half), 2 * t + half, "v_y", 2 * t + half + 1) for t in range(NT) for half in range(2)]
    g += [(("yT", t, half), 2 * t + half, "a_yT", 2 * t + half + 1) for t in range(NT) for half in range(2)]
    g += [("Wo", 4, "x1_ready", 1)]
    f = [("hT", 5, "a_hT", 1), ("fqk", 6, "v_part", 2), ("fv", 7, "v_v9", 1)]
    f += [(("rep", c), 5 + c % 3, "a_QK6", 2 * c + 2) for c in range(NC)]
    f += [(("max", h), 5 + h % 3, "v_mx", h + 1) for h in range(FH)]
    f += [(("mrow", c), 5 + c % 3, "v_mrow", 1 if c == 0 else NC // 2) for c in range(NC // 2)]
    f += [("pv", 7, "v_ctx", 2)] + [(("st", h), 5 + h % 2, "a_pT", h + 1) for h in range(FH)]
    f += [("ctxT", 5, "a_ctxT", 1), ("fWo", 6, "v_x2", 1), ("mT", 5, "a_hT", 2), ("router", 6, "v_lg", 2),
          ("wT", 7, "v_wT", 1), ("b2", 5, "v_moe", 1)]
    for e in range(NE):
        f += [(("h1", e, 0), 5, "a_h1", 2 * e + 1), (("h1", e, 1), 6, "a_h1", 2 * e + 2),
              (("y", e), 7, "v_moe", e + 2)]
    return g + f


OWN_SIGNAL = {"sums", "pv"}


def program(nc, a, out):
    B = a["x"].shape[0]
    table = bank_uses()
    signals = {}

    with ExitStack() as ctx:
        def sb(name, shape, dt=F32):
            return ctx.enter_context(nc.sbuf_tensor(name, shape, dt))

        def signal(name, per):
            signals[name] = Signal(ctx.enter_context(nc.semaphore(name)), per)
            return signals[name]

        def sem(name):
            return ctx.enter_context(nc.semaphore(name))

        banks = [ctx.enter_context(nc.psum_tensor(f"bank{b}", [P, 512], F32)) for b in range(8)]
        bank_full = [sem(f"bank{b}_full") for b in range(8)]
        bank_of = {use: b for use, b, _, _ in table}
        filled, full_per, before, last_of = {}, [0] * 8, {}, {}
        for use, b, name, k in table:
            before[use] = last_of.get(b)
            last_of[b] = (name, k)
            if use not in OWN_SIGNAL:
                full_per[b] += 1
                filled[use] = full_per[b]
        for use, b, _, _ in table:
            if before[use] is None:
                before[use] = (last_of[b][0], last_of[b][1] - 10 ** 6)

        def begun(i, k):
            return k > 0 or not (isinstance(i, int) and i == 0)

        def carry_waits(eng):
            eng.sem_inc(passed, 1)

        def bank(use):
            return banks[bank_of[use]]

        def full_at(i, use):
            return bank_full[bank_of[use]], Signal(None, full_per[bank_of[use]]).at(i, filled[use])

        def emptied(use):
            name, k = before[use]
            return signals[name], k + 10 ** 6 - signals[name].per if k < 0 else k

        def reused(i, use):
            return begun(i, emptied(use)[1])

        def free_at(i, use):
            sig, k = emptied(use)
            return sig.sem, sig.at(i, k)

        def full(use):
            return bank_full[bank_of[use]]

        ident = sb("ident", [P, P])
        identb = sb("identb", [P, P], BF16)
        ident_pad = sb("ident_pad", [P, NT * GW])
        cos = sb("cos", [P, T])
        sin = sb("sin", [P, T])
        head_rows = sb("head_rows", [P, 2])
        alpha_sel = sb("alpha_sel", [P, H * P], BF16)
        q_sel = sb("q_sel", [P, NS, NC, P], BF16)
        k_sel = sb("k_sel", [P, NS, NC, P], BF16)
        k_ones = sb("k_ones", [P, 1])
        earlier = sb("earlier", [P, NE * NE])
        Wqkv = sb("Wqkv", [P, 3, CH])
        Wg = sb("Wg", [P, CH])
        Wo = sb("Wo", [P, NC, HID])
        conv_w = sb("conv_w", [P, 3, NC, KT])
        conv_b = sb("conv_b", [P, 3, NC])
        Wgate = sb("Wgate", [P, 2 * H])
        gate_bias = sb("gate_bias", [P, 2 * H])
        dt_bias = sb("dt_bias", [P, H])
        neg_A = sb("neg_A", [P, H])
        A_log = sb("A_log", [P, H])
        D_bc = sb("D_bc", [P, H])
        onorm = sb("onorm", [P, DH])
        fW = sb("fW", [P, 4, HID])
        ln_gb = sb("ln_gb", [P, 4])
        Wr = sb("Wr", [P, NE])
        W1 = sb("W1", [P, NE, FF])
        b1 = sb("b1", [P, NE, NF])
        W2 = sb("W2", [P, NE, NF, HID])
        b2 = sb("b2", [NE, HID])
        neg_half = sb("neg_half", [P, 1])
        half_c = sb("half_c", [P, 1])
        zeros = sb("zeros", [H, P])

        xin = sb("xin", [P, NT, HID])
        stats = sb("stats", [P, NT, 6])
        mv = sb("mv", [P, NT, 2])
        rstd = sb("rstd", [P, NT])
        xn = sb("xn", [P, NT, HID])
        xnT = sb("xnT", [P, T])
        z = sb("z", [P, NT, 2 * H])
        nabs = sb("nabs", [P, NT, 2 * H])
        zmin = sb("zmin", [P, NT, H])
        eabs = sb("eabs", [P, NT, 2 * H])
        emin = sb("emin", [P, NT, H])
        den = sb("den", [P, NT, 2 * H])
        beta = sb("beta", [P, NT, H])
        lp = sb("lp", [P, NT, H])
        lp2 = sb("lp2", [P, NT, H])
        lpp = sb("lpp", [P, NT, H])
        alpha = sb("alpha", [P, NT, H])
        al1 = sb("al1", [H, NT, P], BF16)
        alr = sb("alr", [H, NT, P])
        al2 = sb("al2", [H, NT, P], BF16)
        alpha3 = sb("alpha3", [P, NT, GW], BF16)
        GT = sb("GT", [H, GW])
        Gc = sb("Gc", [P, 2, H])
        QK = sb("QK", [P, NC, 2, T])
        sk = sb("sk", [P, NT, 3, H])
        rk2 = sb("rk2", [P, NT, H])
        nrm = sb("nrm", [P, NT, H])
        es = sb("es", [P, NT, H])
        dd = sb("dd", [P, NT, H])
        fac = sb("fac", [P, H])
        V = sb("V", [P, NT, H, DH])
        Gam = sb("Gam", [P, H, NT * GW])
        NP = sb("NP", [P, NU, 2, P])
        tmpb = sb("tmpb", [P, SB * SB // 4])
        Z = sb("Z", [P, NU, 2 * SB])
        Kt = sb("Kt", [P, H, DH])
        S = sb("S", [P, NC, DH])
        ms = sb("ms", [P, NT, H])

        def over(tile, n, shape):
            letters = "abcd"[:len(tile.shape) - 1]
            flat = tile[:].rearrange(f"p {' '.join(letters)} -> p ({' '.join(letters)})")
            size = int(np.prod(shape))
            names = "uvw"[:len(shape)]
            return flat[:, 1024 * n:1024 * n + size].rearrange(
                f"p ({' '.join(names)}) -> p {' '.join(names)}", **dict(zip(names, shape)))

        Dg = over(Gam, 0, [SB, NU])
        Eb = over(Gam, 1, [SB, SB])
        X = over(Gam, 2, [SB, SB])
        XB = over(Gam, 3, [SB, NU])
        O = over(QK, 0, [NT, H, DH])
        yT = over(QK, 2, [NT, NC, P])
        T1 = over(Gam, 0, [NU, SB])
        R = over(Gam, 1, [H, DH])
        W = over(Gam, 2, [H, DH])
        Dv = over(Gam, 3, [H, DH])
        acc = over(NP, 0, [2, 2, T])
        qs = over(NP, 1, [2, 2, T])
        rot = over(NP, 2, [2, 2, T])
        qc = over(NP, 3, [2, 2, T])
        vs = over(NP, 4, [NC, T])
        sq = over(NP, 6, [2, 3, T])
        fo = sb("fo", [P, NT, H])
        x1 = sb("x1", [P, NT, HID])

        fstats = sb("fstats", [P, NT, 6])
        fmv = sb("fmv", [P, NT, 2])
        frstd = sb("frstd", [P, NT])
        xf = sb("xf", [P, NT, HID])
        hn = sb("hn", [P, NT, HID])
        hT = sb("hT", [P, T])
        v9 = sb("v9", [P, NT, FH, FD + 1])
        part = sb("part", [P, NS, 2, T], BF16)
        QK6 = sb("QK6", [P, NC, 2, T], BF16)
        mx = sb("mx", [P, NT, FH])
        mrest = sb("mrest", [P, NT, FH])
        mpart = sb("mpart", [P, NS, NT, FH], BF16)
        mpad = sb("mpad", [P, NT, FH, DH], BF16)
        pT = sb("pT", [P, 2, NT, T])
        prest = pT[:, 1]
        rec = sb("rec", [P, NT, FH])
        ctxn = sb("ctxn", [P, NT, HID])
        ctxT = sb("ctxT", [P, T])
        x2 = sb("x2", [P, NT, HID])
        mT = sb("mT", [P, T])
        lg = sb("lg", [P, NT, NE])
        lmax = sb("lmax", [P, NT])
        ex = sb("ex", [P, NT, NE])
        gt = sb("gt", [P, NT, NE, NE])
        eq = sb("eq", [P, NT, NE, NE])
        rank = sb("rank", [P, NT, NE])
        wsel = sb("wsel", [P, NT, NE])
        wden = sb("wden", [P, NT])
        wT = sb("wT", [NE, T])
        h1 = QK6[:].bitcast(F32).rearrange("p (e f) a t -> p e f (a t)", e=2)
        moe = sb("moe", [P, NT, HID])

        loaded = sem("weights_loaded")
        pool_consts = sem("pool_constants_ready")
        act_consts = sem("act_constants_ready")
        vec_consts = sem("vector_constants_ready")
        passed = sem("waits_passed")
        x_in = Signal(sem("x_in"), 16)
        out_stored = Signal(sem("out_stored"), 16)
        x1_ready = signal("x1_ready", 1)
        v_ln = signal("v_ln", 5)
        p_rstd = signal("p_rstd", 1)
        xnT_ready = signal("xnT_ready", 1)
        v_gate = signal("v_gate", 20)
        a_gate = signal("a_gate", 3)
        v_alpha = signal("v_alpha", 7)
        v_Gc = signal("v_Gc", 1)
        a_acc = signal("a_acc", NCONV)
        v_conv = signal("v_conv", 6 * NCONV)
        a_silu = signal("a_silu", NCONV)
        v_rot = signal("v_rot", NC)
        p_sq = signal("p_sq", NC)
        sums_done = signal("sums_done", NC)
        p_rope = signal("p_rope", 2 * NC)
        v_QK = signal("v_QK", NC)
        v_sum = signal("v_sum", 6)
        p_nrm = signal("p_nrm", 1)
        v_V = signal("v_V", 4)
        v_Gam = signal("v_Gam", H)
        v_NP = signal("v_NP", H)
        a_diag = signal("a_diag", 2)
        p_blk = signal("p_blk", 4)
        v_blk = signal("v_blk", 1 + 2 * (SB - 1) + 5)
        a_T1 = signal("a_T1", 2)
        a_Z = signal("a_Z", 2)
        v_Kt = signal("v_Kt", 3)
        a_W = signal("a_W", 8)
        v_R = signal("v_R", 6)
        a_S = signal("a_S", 1)
        p_R1 = signal("p_R1", 2)
        p_Dv = signal("p_Dv", 4)
        v_QS = signal("v_QS", 2)
        v_O = signal("v_O", 4)
        a_osq = signal("a_osq", 1)
        v_ms = signal("v_ms", 3)
        p_f = signal("p_f", 1)
        p_on = signal("p_on", 4)
        a_sg = signal("a_sg", 2)
        v_y = signal("v_y", 4)
        a_yT = signal("a_yT", 4)
        f_ln = signal("f_ln", 15)
        fp_rstd = signal("fp_rstd", 3)
        a_hT = signal("a_hT", 2)
        v_part = signal("v_part", 4)
        v_v9 = signal("v_v9", 1)
        a_QK6 = signal("a_QK6", 2 * NC)
        v_mx = signal("v_mx", FH)
        v_mp = signal("v_mp", 5)
        v_mrow = signal("v_mrow", NC // 2)
        a_pT = signal("a_pT", FH)
        pv_done = signal("pv_done", FH)
        v_ctx = signal("v_ctx", 2)
        a_ctxT = signal("a_ctxT", 1)
        v_x2 = signal("v_x2", 1)
        p_xs = signal("p_xs", 1)
        v_lg = signal("v_lg", 2)
        a_ex = signal("a_ex", 1)
        v_w = signal("v_w", 9)
        v_wT = signal("v_wT", 1)
        a_h1 = signal("a_h1", 2 * NE)
        v_moe = signal("v_moe", 1 + NE)

        block = ctx.enter_context(nc.Block())

        stage = NP[:, :, :, :].rearrange("p u a b -> p (u a b)")
        n_q = NS * NC * P
        loads = [(ident[:], a["c_ident"]), (ident_pad[:], a["c_ident_pad"]), 
                 (cos[:], a["c_cos"]), (sin[:], a["c_sin"]), (head_rows[:], a["c_head_rows"]),
                 (k_ones[:], a["c_k_ones"]), (earlier[:], a["c_earlier"]),
                 (stage[:, 0:H * P], a["c_alpha_sel"]),
                 (stage[:, H * P:H * P + n_q], a["c_q_sel"]),
                 (stage[:, H * P + n_q:H * P + 2 * n_q], a["c_k_sel"]),
                 (Wqkv[:, 0, :], a["Wq"]), (Wqkv[:, 1, :], a["Wk"]), (Wqkv[:, 2, :], a["Wv"]),
                 (Wg[:], a["Wg"]), (Wo[:], a["Wo"].rearrange("(c p) n -> p c n", p=P)),
                 (conv_w[:], a["conv_w"]), (conv_b[:], a["conv_b"]),
                 (Wgate[:, 0:H], a["bw"]), (Wgate[:, H:2 * H], a["gkw"]),
                 (gate_bias[:, 0:H], a["bb"].partition_broadcast(P)),
                 (gate_bias[:, H:2 * H], a["gkb"].partition_broadcast(P)),
                 (dt_bias[:], a["dt_bias"].partition_broadcast(P)),
                 (A_log[:], a["A_log"].partition_broadcast(P)),
                 (D_bc[:], a["D_param"].partition_broadcast(P)),
                 (onorm[:], a["onorm_w"].partition_broadcast(P)),
                 (fW[:, 0, :], a["fWq"]), (fW[:, 1, :], a["fWk"]), (fW[:, 2, :], a["fWv"]), (fW[:, 3, :], a["fWo"]),
                 (ln_gb[:, 0:1], a["ln1_g"]), (ln_gb[:, 1:2], a["ln1_b"]),
                 (ln_gb[:, 2:3], a["ln2_g"]), (ln_gb[:, 3:4], a["ln2_b"]),
                 (Wr[:], a["fWg"]), (W1[:], a["W1"].rearrange("e d f -> d e f")), (b1[:], a["b1"]),
                 (W2[:], a["W2"].rearrange("e (c p) d -> p e c d", p=P)), (b2[:], a["b2"])]

        def bc(ap, n):
            sh = list(ap.shape)
            return ap.unsqueeze(len(sh)).to_broadcast(sh + [n])

        def x_rows(i):
            return a["x"][bass.ds(i, 1)].rearrange("a (t p) d -> p (a t) d", p=P)

        def out_rows(i):
            return out[bass.ds(i, 1)].rearrange("a (t p) d -> p (a t) d", p=P)

        HALF = [slice(0, 8), slice(8, 16)]
        PARITY = [slice(0, H, 2), slice(1, H, 2)]
        ROWS = [slice(SB * q, SB * q + SB) for q in range(P // SB)]
        TOK = [slice(t * P, t * P + P) for t in range(NT)]

        def head_rows_of(h):
            return slice((h % 2) * DH, (h % 2) * DH + DH)

        def pair(tile):
            return tile[:].rearrange("p (a t) -> p a t", a=2)

        def by_head(tile):
            return tile[:].rearrange("p (h d) -> p h d", h=8)

        def by_unit(tile):
            return tile[:].rearrange("p (u s) -> p u s", u=16)

        @block.sync
        def _(sp):
            for dst, src in loads:
                sp.dma_start(dst, src).then_inc(loaded, 16)
            sp.dma_start(xin[:], x_rows(0)).then_inc(x_in.sem, 16)

            def batch(i, last):
                if not last:
                    sp.wait_ge(x1_ready.sem, x1_ready.at(i, 1))
                    sp.dma_start(xin[:], x_rows(i + 1)).then_inc(x_in.sem, 16)
                sp.wait_ge(v_moe.sem, v_moe.at(i, v_moe.per))
                sp.dma_start(out_rows(i), moe[:]).then_inc(out_stored.sem, 16)

            batch(0, B == 1)
            if B > 2:
                with sp.Fori(1, B - 1) as i:
                    batch(i, False)
            if B > 1:
                batch(B - 1, True)
            sp.wait_ge(out_stored.sem, out_stored.at(B, 0))

        @block.gpsimd
        def _(pool):
            g = nc.gpsimd
            g.memset(neg_half[:], -0.5).then_inc(pool_consts, 1)
            g.memset(half_c[:], 0.5).then_inc(pool_consts, 1)
            g.memset(alpha3[:], 0.0).then_inc(pool_consts, 1)
            g.memset(Z[:], 0.0).then_inc(pool_consts, 1)
            g.memset(mpad[:], 0.0).then_inc(pool_consts, 1)
            g.memset(v9[:], 1.0).then_inc(pool_consts, 1)
            g.memset(zeros[:], 0.0).then_inc(pool_consts, 1)
            g.memset(GT[:], 1.0).then_inc(pool_consts, 1)
            pool.wait_ge(pool_consts, 8)
            pool.wait_ge(loaded, 16 * len(loads))

            def gdn(i):
                pool.wait_ge(v_ln.sem, v_ln.at(i, 3))
                g.tensor_tensor(rstd[:], mv[:, :, 1], neg_half[:, 0:1].to_broadcast([P, NT]),
                                ALU.pow).then_inc(p_rstd.sem, 1)
                for c in range(NC):
                    b = c % 2
                    pool.wait_ge(a_silu.sem, a_silu.at(i, c + 1))
                    if begun(i, c - 1):
                        pool.wait_ge(sums_done.sem, sums_done.at(i, c - 1))
                    g.tensor_tensor(sq[:, b, 0:2, :], qs[:, b], qs[:, b], ALU.mult)
                    g.tensor_tensor(sq[:, b, 2, :], qs[:, b, 0, :], qs[:, b, 1, :], ALU.mult).then_inc(p_sq.sem, 1)
                    if begun(i, c - 1):
                        pool.wait_ge(v_QK.sem, v_QK.at(i, c - 1))
                    g.tensor_tensor(qc[:, b], qs[:, b], cos[:].unsqueeze(1).to_broadcast([P, 2, T]),
                                    ALU.mult).then_inc(p_rope.sem, 1)
                    pool.wait_ge(v_rot.sem, v_rot.at(i, c + 1))
                    g.tensor_tensor(rot[:, b], rot[:, b], sin[:].unsqueeze(1).to_broadcast([P, 2, T]),
                                    ALU.mult).then_inc(p_rope.sem, 1)
                pool.wait_ge(v_sum.sem, v_sum.at(i, 2))
                g.tensor_tensor(nrm[:], sk[:, :, 1, :], half_c[:, 0:1].unsqueeze(1).to_broadcast([P, NT, H]),
                                ALU.pow).then_inc(p_nrm.sem, 1)
                pool.wait_ge(v_Kt.sem, v_Kt.at(i, 1))
                carry_waits(pool)
                g.memset(X, 0.0).then_inc(p_blk.sem, 1)
                pool.wait_ge(p_blk.sem, p_blk.at(i, 1))
                carry_waits(pool)
                g.memset(X.rearrange("p t c -> p (t c)")[:, ::SB + 1], 1.0).then_inc(p_blk.sem, 1)
                for q in (2, 3):
                    pool.wait_ge(p_blk.sem, p_blk.at(i, q))
                    carry_waits(pool)
                    g.tensor_copy(Dg[ROWS[q]], NP[ROWS[q], :, 1, ROWS[q]].rearrange("p u t -> p t u"))\
                        .then_inc(p_blk.sem, 1)
                pool.wait_ge(p_blk.sem, p_blk.at(i, 4))
                pool.wait_ge(v_sum.sem, v_sum.at(i, 6))
                pool.wait_ge(a_T1.sem, a_T1.at(i, 2))
                g.tensor_tensor(Dv[:], V[:, 0], bc(dd[:, 0, :], DH), ALU.mult).then_inc(p_Dv.sem, 1)
                for half in range(2):
                    pool.wait_ge(v_R.sem, v_R.at(i, 3 + half))
                    g.tensor_tensor(R[:, PARITY[half], :], V[:, 1, PARITY[half], :], R[:, PARITY[half], :],
                                    ALU.subtract).then_inc(p_R1.sem, 1)
                pool.wait_ge(v_O.sem, v_O.at(i, 2))
                g.tensor_tensor(Dv[:], V[:, 1], bc(dd[:, 1, :], DH), ALU.mult).then_inc(p_Dv.sem, 1)
                pool.wait_ge(p_Dv.sem, p_Dv.at(i, 2))
                for half in range(2):
                    pool.wait_ge(v_QS.sem, v_QS.at(i, half + 1))
                    g.tensor_tensor(Dv[:, PARITY[half], :], Dv[:, PARITY[half], :], Kt[:, PARITY[half], :],
                                    ALU.add).then_inc(p_Dv.sem, 1)
                pool.wait_ge(v_ms.sem, v_ms.at(i, 3))
                g.tensor_tensor(fo[:], ms[:], neg_half[:, 0:1].unsqueeze(1).to_broadcast([P, NT, H]),
                                ALU.pow).then_inc(p_f.sem, 1)
                pool.wait_ge(p_f.sem, p_f.at(i, 1))
                for t in range(NT):
                    g.tensor_tensor(O[:, t], O[:, t], bc(fo[:, t, :], DH), ALU.mult).then_inc(p_on.sem, 1)
                    pool.wait_ge(p_on.sem, p_on.at(i, 2 * t + 1))
                    g.tensor_tensor(O[:, t], O[:, t], onorm[:].unsqueeze(1).to_broadcast([P, H, DH]),
                                    ALU.mult).then_inc(p_on.sem, 1)

            def ffn(i):
                for n in range(3):
                    pool.wait_ge(f_ln.sem, f_ln.at(i, 5 * n + 3))
                    g.tensor_tensor(frstd[:], fmv[:, :, 1], neg_half[:, 0:1].to_broadcast([P, NT]),
                                    ALU.pow).then_inc(fp_rstd.sem, 1)
                g.tensor_tensor(x1[:], x1[:], x2[:], ALU.add).then_inc(p_xs.sem, 1)

            gdn(0)
            ffn(0)
            if B > 1:
                with pool.Fori(1, B) as i:
                    gdn(i)
                    ffn(i)

        @block.scalar
        def _(act):
            s = nc.scalar
            act.wait_ge(loaded, 16 * len(loads))
            s.copy(identb[:], ident[:]).then_inc(act_consts, 1)
            s.copy(alpha_sel[:], stage[:, 0:H * P]).then_inc(act_consts, 1)
            s.copy(q_sel[:].rearrange("p a b c -> p (a b c)"), stage[:, H * P:H * P + n_q]).then_inc(act_consts, 1)
            s.copy(k_sel[:].rearrange("p a b c -> p (a b c)"), stage[:, H * P + n_q:H * P + 2 * n_q])\
                .then_inc(act_consts, 1)
            s.activation(neg_A[:], A_log[:], ACT.Exp).then_inc(act_consts, 1)
            act.wait_ge(act_consts, 5)
            s.mul(neg_A[:], neg_A[:], -1.0).then_inc(act_consts, 1)

            def first_tap(i, n):
                use = ("qk", n) if n < NC else ("v", n - NC)
                which = ((0, n), (1, n)) if n < NC else ((2, 2 * (n - NC)), (2, 2 * (n - NC) + 1))
                act.wait_ge(*full_at(i, use))
                ps = pair(bank(use))
                if begun(i, n - 1):
                    act.wait_ge(a_silu.sem, a_silu.at(i, n - 1))
                for m, (kind, c) in enumerate(which):
                    ins = s.activation(acc[:, n % 2, m, :], ps[:, m, :], ACT.Identity,
                                       bias=conv_b[:, kind, c:c + 1], scale=conv_w[:, kind, c, PAD:KT])
                ins.then_inc(a_acc.sem, 1)

            def silu(i, n):
                act.wait_ge(v_conv.sem, v_conv.at(i, 6 * (n + 1)))
                if n < NC:
                    if begun(i, 2 * n - 3):
                        act.wait_ge(p_rope.sem, p_rope.at(i, 2 * n - 3))
                    if begun(i, n - 1):
                        act.wait_ge(v_rot.sem, v_rot.at(i, n - 1))
                    s.activation(qs[:, n % 2], acc[:, n % 2], ACT.Silu).then_inc(a_silu.sem, 1)
                else:
                    m = n - NC
                    s.activation(vs[:, 2 * m:2 * m + 2, :], acc[:, n % 2], ACT.Silu).then_inc(a_silu.sem, 1)

            def gdn(i):
                act.wait_ge(*full_at(i, "xT"))
                ps = bank("xT")
                s.copy(xnT[:], ps[:, 0:T]).then_inc(xnT_ready.sem, 1)
                act.wait_ge(v_gate.sem, v_gate.at(i, 3))
                s.activation(eabs[:], nabs[:], ACT.Exp).then_inc(a_gate.sem, 1)
                s.activation(emin[:], zmin[:], ACT.Exp).then_inc(a_gate.sem, 1)
                for n in range(NCONV + 1):
                    if n < NCONV:
                        first_tap(i, n)
                    if n == 1:
                        act.wait_ge(v_gate.sem, v_gate.at(i, 20))
                        s.activation(alpha[:], lpp[:], ACT.Exp).then_inc(a_gate.sem, 1)
                    if n >= 1:
                        silu(i, n - 1)
                act.wait_ge(v_Kt.sem, v_Kt.at(i, 1))
                for q in (0, 1):
                    s.copy(Dg[ROWS[q]], NP[ROWS[q], :, 1, ROWS[q]].rearrange("p u t -> p t u")).then_inc(a_diag.sem, 1)
                for half in range(2):
                    act.wait_ge(*full_at(i, ("join1", half)))
                    ps = bank(("join1", half))
                    for q in (1, 3):
                        ins = s.copy(T1[ROWS[q], 16 * half:16 * half + 16, :], by_unit(ps)[ROWS[q]])
                    ins.then_inc(a_T1.sem, 1)
                for half in range(2):
                    act.wait_ge(*full_at(i, ("join2", half)))
                    ps = bank(("join2", half))
                    for q in (0, 2):
                        ins = s.mul(Z[ROWS[q], 16 * half:16 * half + 16, SB:2 * SB], by_unit(ps)[ROWS[q]], -1.0)
                    ins.then_inc(a_Z.sem, 1)
                for t in range(NT):
                    for what, rows in (("top", slice(0, DH)), ("low", slice(DH, P))):
                        for half in range(2):
                            act.wait_ge(*full_at(i, (what, t, half)))
                            ps = bank((what, t, half))
                            if t:
                                act.wait_ge(*full_at(i, ("o", 0, 1)))
                            s.copy(W[rows, HALF[half], :], by_head(ps)[rows]).then_inc(a_W.sem, 1)
                    if t == 0:
                        act.wait_ge(*full_at(i, "S"))
                        ps = bank("S")
                        s.copy(S[:], by_head(ps)).then_inc(a_S.sem, 1)
                act.wait_ge(v_O.sem, v_O.at(i, 4))
                s.activation(V[:], O[:], ACT.Square).then_inc(a_osq.sem, 1)
                for t in range(NT):
                    act.wait_ge(p_on.sem, p_on.at(i, 2 * t + 2))
                    s.activation(O[:, t], O[:, t], ACT.Silu).then_inc(a_sg.sem, 1)
                for t in range(NT):
                    for half in range(2):
                        act.wait_ge(*full_at(i, ("yT", t, half)))
                        ps = bank(("yT", t, half))
                        s.copy(yT[:, t, 4 * half:4 * half + 4, :], ps[:].rearrange("p (c k) -> p c k", c=4))\
                            .then_inc(a_yT.sem, 1)

            def ffn(i):
                act.wait_ge(*full_at(i, "hT"))
                ps = bank("hT")
                s.activation(hT[:], ps[:, 0:T], ACT.Identity, bias=ln_gb[:, 1:2], scale=ln_gb[:, 0:1])\
                    .then_inc(a_hT.sem, 1)
                for c in range(NC):
                    act.wait_ge(*full_at(i, ("rep", c)))
                    ps = pair(bank(("rep", c)))
                    s.copy(QK6[:, c, 0, :], ps[:, 0, :]).then_inc(a_QK6.sem, 1)
                    s.activation(QK6[:, c, 1, :], ps[:, 1, :], ACT.Identity, bias=k_ones[:, 0:1])\
                        .then_inc(a_QK6.sem, 1)
                for h in range(FH):
                    act.wait_ge(*full_at(i, ("st", h)))
                    ps = bank(("st", h))
                    if begun(i, h - 1):
                        act.wait_ge(pv_done.sem, pv_done.at(i, h - 1))
                    s.activation(pT[:, h % 2], pair(ps), ACT.Exp, scale=float(FD) ** -0.5).then_inc(a_pT.sem, 1)
                act.wait_ge(*full_at(i, "ctxT"))
                ps = bank("ctxT")
                s.copy(ctxT[:], ps[:, 0:T]).then_inc(a_ctxT.sem, 1)
                act.wait_ge(*full_at(i, "mT"))
                ps = bank("mT")
                s.activation(mT[:], ps[:, 0:T], ACT.Identity, bias=ln_gb[:, 3:4], scale=ln_gb[:, 2:3])\
                    .then_inc(a_hT.sem, 1)
                act.wait_ge(v_lg.sem, v_lg.at(i, 2))
                s.activation(ex[:], lg[:], ACT.Exp).then_inc(a_ex.sem, 1)
                for e in range(NE):
                    for j in range(2):
                        act.wait_ge(*full_at(i, ("h1", e, j)))
                        ps = pair(bank(("h1", e, j)))
                        if e >= 2:
                            act.wait_ge(*full_at(i, ("y", e - 2)))
                        for m in range(2):
                            f = 2 * j + m
                            ins = s.activation(h1[:, e % 2, f, :], ps[:, m, :], ACT.Gelu_apprx_tanh,
                                               bias=b1[:, e, f:f + 1])
                        ins.then_inc(a_h1.sem, 1)

            gdn(0)
            ffn(0)
            if B > 1:
                with act.Fori(1, B) as i:
                    gdn(i)
                    ffn(i)

        @block.tensor
        def _(pe):
            mm = nc.tensor.matmul

            def product(out_, lhsT, rhs, first=True, last=True):
                return mm(out_, lhsT, rhs, start=first, stop=last)

            def turn(out_, in_, n=P):
                return nc.tensor.transpose(out_, in_, ident[0:n, 0:n])

            pe.wait_ge(loaded, 16 * len(loads))
            pe.wait_ge(pool_consts, 8)
            pe.wait_ge(act_consts, 6)

            def sums(i, c):
                if c == 0 and reused(i, "sums"):
                    pe.wait_ge(*free_at(i, "sums"))
                ps = bank("sums")
                dst = ps[:, 0:NT * 3 * H].rearrange("p (t a h) -> p t a h", t=NT, a=3)
                pe.wait_ge(p_sq.sem, p_sq.at(i, c + 1))
                for t in range(NT):
                    for kind in range(3):
                        ins = product(dst[:, t, kind, 2 * c:2 * c + 2], sq[:, c % 2, kind, TOK[t]], head_rows[:])
                ins.then_inc(sums_done.sem, 1)

            def gdn(i):
                pe.wait_ge(v_ln.sem, v_ln.at(i, 5))
                if reused(i, "xT"):
                    pe.wait_ge(*free_at(i, "xT"))
                ps = bank("xT")
                for t in range(NT):
                    ins = turn(ps[:, TOK[t]], xn[:, t, :])
                ins.then_inc(full("xT"), 1)
                pe.wait_ge(xnT_ready.sem, xnT_ready.at(i, 1))
                if reused(i, "gate"):
                    pe.wait_ge(*free_at(i, "gate"))
                ps = bank("gate")
                for t in range(NT):
                    ins = product(ps[:, t * 2 * H:(t + 1) * 2 * H], xnT[:, TOK[t]], Wgate[:])
                ins.then_inc(full("gate"), 1)
                for n in range(NCONV + 2):
                    if n == 4:
                        pe.wait_ge(a_gate.sem, a_gate.at(i, 3))
                        if reused(i, "alphaT"):
                            pe.wait_ge(*free_at(i, "alphaT"))
                        ps = bank("alphaT")
                        for t in range(NT):
                            ins = turn(ps[0:H, TOK[t]], alpha[:, t, :])
                        ins.then_inc(full("alphaT"), 1)
                    if n == 6:
                        pe.wait_ge(v_alpha.sem, v_alpha.at(i, 7))
                        if reused(i, "GT"):
                            pe.wait_ge(*free_at(i, "GT"))
                        ps = bank("GT")
                        carry_waits(pe)
                        turn(ps[:, 0:H], GT[:, 1:GW], H)
                        turn(ps[:, H:2 * H], GT[:, 0:P], H).then_inc(full("GT"), 1)
                    if n < NCONV:
                        use = ("qk", n) if n < NC else ("v", n - NC)
                        which = ((0, n), (1, n)) if n < NC else ((2, 2 * (n - NC)), (2, 2 * (n - NC) + 1))
                        if reused(i, use):
                            pe.wait_ge(*free_at(i, use))
                        ps = pair(bank(use))
                        for m, (kind, c) in enumerate(which):
                            ins = product(ps[:, m, :], Wqkv[:, kind, c * P:(c + 1) * P], xnT[:])
                        ins.then_inc(full(use), 1)
                    if 2 <= n < NC + 2:
                        sums(i, n - 2)
                for half in range(2):
                    pe.wait_ge(a_silu.sem, a_silu.at(i, NC + 2 * half + 2))
                    for t in range(NT):
                        if reused(i, ("vT", t, half)):
                            pe.wait_ge(*free_at(i, ("vT", t, half)))
                        ps = bank(("vT", t, half))
                        for c in range(4):
                            ins = turn(ps[:, c * P:(c + 1) * P], vs[:, 4 * half + c, TOK[t]])
                        ins.then_inc(full(("vT", t, half)), 1)
                for h in range(H):
                    c, rows = h // 2, head_rows_of(h)
                    if reused(i, ("alpha", h)):
                        pe.wait_ge(*free_at(i, ("alpha", h)))
                    ps = bank(("alpha", h))
                    pe.wait_ge(v_alpha.sem, v_alpha.at(i, 7))
                    product(ps[:, 0:NT * GW], alpha_sel[:, h * P:(h + 1) * P],
                            alpha3[:].rearrange("p t w -> p (t w)")).then_inc(full(("alpha", h)), 1)
                    if reused(i, ("kk", h)):
                        pe.wait_ge(*free_at(i, ("kk", h)))
                    ps = bank(("kk", h))
                    pe.wait_ge(v_QK.sem, v_QK.at(i, c + 1))
                    for t in range(NT):
                        ins = product(ps[:, t * T:(t + 1) * T].rearrange("p (a k) -> p a k", a=2),
                                      QK[rows, c, 1, TOK[t]], QK[rows, c, :, TOK[t]])
                    ins.then_inc(full(("kk", h)), 1)
                for half in range(2):
                    if reused(i, ("kT", half)):
                        pe.wait_ge(*free_at(i, ("kT", half)))
                    ps = bank(("kT", half))
                    for c in range(4):
                        ins = turn(ps[:, c * P:(c + 1) * P], QK[:, 4 * half + c, 1, 0:P])
                    ins.then_inc(full(("kT", half)), 1)
                pe.wait_ge(v_blk.sem, v_blk.at(i, v_blk.per))
                for half in range(2):
                    if reused(i, ("join1", half)):
                        pe.wait_ge(*free_at(i, ("join1", half)))
                    ps = bank(("join1", half))
                    carry_waits(pe)
                    for u in range(16):
                        for q in (0, 2):
                            ins = product(by_unit(ps)[ROWS[q + 1], u, :], NP[ROWS[q], 16 * half + u, 1, ROWS[q + 1]],
                                          XB[ROWS[q], :, 16 * half + u])
                    ins.then_inc(full(("join1", half)), 1)
                for half in range(2):
                    if reused(i, ("join2", half)):
                        pe.wait_ge(*free_at(i, ("join2", half)))
                    ps = bank(("join2", half))
                    pe.wait_ge(a_T1.sem, a_T1.at(i, half + 1))
                    carry_waits(pe)
                    for u in range(16):
                        for q in (0, 2):
                            ins = product(by_unit(ps)[ROWS[q], u, :], T1[ROWS[q + 1], 16 * half + u, :],
                                          Z[ROWS[q + 1], 16 * half + u, SB:2 * SB])
                    ins.then_inc(full(("join2", half)), 1)
                pe.wait_ge(v_V.sem, v_V.at(i, 4))
                top, low = slice(0, DH), slice(DH, P)
                for t in range(NT):
                    right = V[:, 0] if t == 0 else R[:]
                    for half in range(2):
                        if reused(i, ("top", t, half)):
                            pe.wait_ge(*free_at(i, ("top", t, half)))
                        ps = bank(("top", t, half))
                        if t:
                            pe.wait_ge(p_R1.sem, p_R1.at(i, 2))
                        carry_waits(pe)
                        for k in range(8):
                            h = 8 * half + k
                            ins = product(by_head(ps)[top, k, :], Z[top, t * H + h, :], right[top, h, :])
                        ins.then_inc(full(("top", t, half)), 1)
                    for half in range(2):
                        if reused(i, ("cross", t, half)):
                            pe.wait_ge(*free_at(i, ("cross", t, half)))
                        ps = bank(("cross", t, half))
                        pe.wait_ge(a_W.sem, a_W.at(i, 4 * t + half + 1))
                        carry_waits(pe)
                        for k in range(8):
                            h = 8 * half + k
                            ins = product(by_head(ps)[low, k, :], NP[top, t * H + h, 1, DH:P], W[top, h, :])
                        ins.then_inc(full(("cross", t, half)), 1)
                    for half in range(2):
                        if reused(i, ("low", t, half)):
                            pe.wait_ge(*free_at(i, ("low", t, half)))
                        ps = bank(("low", t, half))
                        pe.wait_ge(v_R.sem, v_R.at(i, 4 * t + half + 1))
                        carry_waits(pe)
                        for k in range(8):
                            h = 8 * half + k
                            ins = product(by_head(ps)[low, k, :], Z[low, t * H + h, :], R[low, h, :])
                        ins.then_inc(full(("low", t, half)), 1)
                    if t == 0:
                        if reused(i, "S"):
                            pe.wait_ge(*free_at(i, "S"))
                        ps = bank("S")
                        pe.wait_ge(v_Kt.sem, v_Kt.at(i, 3))
                        pe.wait_ge(a_W.sem, a_W.at(i, 4))
                        for h in range(H):
                            ins = product(by_head(ps)[head_rows_of(h), h // 2, :], Kt[:, h, :], W[:, h, :])
                        ins.then_inc(full("S"), 1)
                        for what, kind in (("KS", 1), ("QS", 0)):
                            for half in range(2):
                                pe.wait_ge(a_S.sem, a_S.at(i, 1))
                                if reused(i, (what, half)):
                                    pe.wait_ge(*free_at(i, (what, half)))
                                ps = bank((what, half))
                                for k in range(8):
                                    h = 2 * k + half
                                    ins = product(by_head(ps)[:, k, :], QK[head_rows_of(h), h // 2, kind, TOK[1]],
                                                  S[head_rows_of(h), h // 2, :])
                                ins.then_inc(full((what, half)), 1)
                    for half in range(2):
                        if reused(i, ("o", t, half)):
                            pe.wait_ge(*free_at(i, ("o", t, half)))
                        ps = bank(("o", t, half))
                        pe.wait_ge(a_W.sem, a_W.at(i, 4 * t + half + 3))
                        for k in range(8):
                            h = 8 * half + k
                            ins = product(by_head(ps)[:, k, :], NP[:, t * H + h, 0, :], W[:, h, :])
                        ins.then_inc(full(("o", t, half)), 1)
                for t in range(NT):
                    for half in range(2):
                        if reused(i, ("g", t, half)):
                            pe.wait_ge(*free_at(i, ("g", t, half)))
                        ps = bank(("g", t, half))
                        product(ps[:], xnT[:, TOK[t]], Wg[:, half * 512:(half + 1) * 512])\
                            .then_inc(full(("g", t, half)), 1)
                for t in range(NT):
                    for half in range(2):
                        if reused(i, ("yT", t, half)):
                            pe.wait_ge(*free_at(i, ("yT", t, half)))
                        ps = bank(("yT", t, half))
                        for c in range(4):
                            h = 8 * half + 2 * c
                            ins = turn(ps[:, c * P:(c + 1) * P], O[:, t, h:h + 2, :].rearrange("p h d -> p (h d)"))
                        ins.then_inc(full(("yT", t, half)), 1)
                if reused(i, "Wo"):
                    pe.wait_ge(*free_at(i, "Wo"))
                ps = bank("Wo")
                for t in range(NT):
                    pe.wait_ge(a_yT.sem, a_yT.at(i, 2 * t + 2))
                    for c in range(NC):
                        ins = product(ps[:, TOK[t]], yT[:, t, c, :], Wo[:, c, :], c == 0, c == NC - 1)
                ins.then_inc(full("Wo"), 1)

            def ffn(i):
                pe.wait_ge(f_ln.sem, f_ln.at(i, 10))
                if reused(i, "hT"):
                    pe.wait_ge(*free_at(i, "hT"))
                ps = bank("hT")
                for t in range(NT):
                    ins = turn(ps[:, TOK[t]], hn[:, t, :])
                ins.then_inc(full("hT"), 1)
                pe.wait_ge(a_hT.sem, a_hT.at(i, 1))
                if reused(i, "fqk"):
                    pe.wait_ge(*free_at(i, "fqk"))
                ps = pair(bank("fqk"))
                product(ps[:, 0, :], fW[:, 0, :], hT[:])
                product(ps[:, 1, :], fW[:, 1, :], hT[:]).then_inc(full("fqk"), 1)
                if reused(i, "fv"):
                    pe.wait_ge(*free_at(i, "fv"))
                ps = bank("fv")
                for t in range(NT):
                    ins = product(ps[:, TOK[t]], hT[:, TOK[t]], fW[:, 2, :])
                ins.then_inc(full("fv"), 1)
                pe.wait_ge(v_part.sem, v_part.at(i, 4))
                for c in range(NC):
                    if reused(i, ("rep", c)):
                        pe.wait_ge(*free_at(i, ("rep", c)))
                    ps = pair(bank(("rep", c)))
                    for kind, sel in ((0, q_sel), (1, k_sel)):
                        for n in range(NS):
                            ins = product(ps[:, kind, :], sel[:, n, c, :], part[:, n, kind, :], n == 0, n == NS - 1)
                    ins.then_inc(full(("rep", c)), 1)
                for h in range(FH):
                    c, rows = h // 2, head_rows_of(h)
                    pe.wait_ge(a_QK6.sem, a_QK6.at(i, 2 * c + 2))
                    if reused(i, ("max", h)):
                        pe.wait_ge(*free_at(i, ("max", h)))
                    ps = pair(bank(("max", h)))
                    for t in range(NT):
                        ins = product(ps[:, t, :], QK6[rows, c, 0, TOK[t]], QK6[rows, c, 1, :])
                    ins.then_inc(full(("max", h)), 1)
                pe.wait_ge(v_mp.sem, v_mp.at(i, 5))
                for m in range(NC // 2):
                    if reused(i, ("mrow", m)):
                        pe.wait_ge(*free_at(i, ("mrow", m)))
                    ps = pair(bank(("mrow", m)))
                    for j in range(2):
                        c = 2 * m + j
                        for t in range(NT):
                            ins = product(ps[:, j, TOK[t]],
                                          mpad[:, t, 2 * c:2 * c + 2, :].rearrange("p h d -> p (h d)"), identb[:])
                    ins.then_inc(full(("mrow", m)), 1)
                pe.wait_ge(v_v9.sem, v_v9.at(i, 1))
                if reused(i, "pv"):
                    pe.wait_ge(*free_at(i, "pv"))
                pv = bank("pv")[:, 0:NT * FH * (FD + 1)].rearrange("p (t h d) -> p t h d", t=NT, h=FH)
                for h in range(FH + 1):
                    if h < FH:
                        c, rows = h // 2, head_rows_of(h)
                        if reused(i, ("st", h)):
                            pe.wait_ge(*free_at(i, ("st", h)))
                        ps = pair(bank(("st", h)))
                        for kt in range(NT):
                            ins = product(ps[:, kt, :], QK6[rows, c, 1, TOK[kt]], QK6[rows, c, 0, :])
                        ins.then_inc(full(("st", h)), 1)
                    if h >= 1:
                        pe.wait_ge(a_pT.sem, a_pT.at(i, h))
                        for t in range(NT):
                            for kt in range(NT):
                                ins = product(pv[:, t, h - 1, :], pT[:, (h - 1) % 2, kt, TOK[t]], v9[:, kt, h - 1, :],
                                              kt == 0, kt == NT - 1)
                        ins.then_inc(pv_done.sem, 1)
                pe.wait_ge(v_ctx.sem, v_ctx.at(i, 2))
                if reused(i, "ctxT"):
                    pe.wait_ge(*free_at(i, "ctxT"))
                ps = bank("ctxT")
                for t in range(NT):
                    ins = turn(ps[:, TOK[t]], ctxn[:, t, :])
                ins.then_inc(full("ctxT"), 1)
                pe.wait_ge(a_ctxT.sem, a_ctxT.at(i, 1))
                if reused(i, "fWo"):
                    pe.wait_ge(*free_at(i, "fWo"))
                ps = bank("fWo")
                for t in range(NT):
                    ins = product(ps[:, TOK[t]], ctxT[:, TOK[t]], fW[:, 3, :])
                ins.then_inc(full("fWo"), 1)
                pe.wait_ge(f_ln.sem, f_ln.at(i, 15))
                if reused(i, "mT"):
                    pe.wait_ge(*free_at(i, "mT"))
                ps = bank("mT")
                for t in range(NT):
                    ins = turn(ps[:, TOK[t]], hn[:, t, :])
                ins.then_inc(full("mT"), 1)
                pe.wait_ge(a_hT.sem, a_hT.at(i, 2))
                if reused(i, "router"):
                    pe.wait_ge(*free_at(i, "router"))
                ps = bank("router")
                for t in range(NT):
                    ins = product(ps[:, t * NE:(t + 1) * NE], mT[:, TOK[t]], Wr[:])
                ins.then_inc(full("router"), 1)
                pe.wait_ge(v_w.sem, v_w.at(i, 9))
                if reused(i, "wT"):
                    pe.wait_ge(*free_at(i, "wT"))
                ps = bank("wT")
                for t in range(NT):
                    ins = turn(ps[0:NE, TOK[t]], wsel[:, t, :])
                ins.then_inc(full("wT"), 1)
                pe.wait_ge(v_wT.sem, v_wT.at(i, 1))
                if reused(i, "b2"):
                    pe.wait_ge(*free_at(i, "b2"))
                ps = bank("b2")
                for t in range(NT):
                    ins = product(ps[:, TOK[t]], wT[:, TOK[t]], b2[:])
                ins.then_inc(full("b2"), 1)
                for e in range(NE + 1):
                    if e < NE:
                        for j in range(2):
                            if reused(i, ("h1", e, j)):
                                pe.wait_ge(*free_at(i, ("h1", e, j)))
                            ps = pair(bank(("h1", e, j)))
                            for m in range(2):
                                f = 2 * j + m
                                ins = product(ps[:, m, :], W1[:, e, f * P:(f + 1) * P], mT[:])
                            ins.then_inc(full(("h1", e, j)), 1)
                    if e >= 1:
                        if reused(i, ("y", e - 1)):
                            pe.wait_ge(*free_at(i, ("y", e - 1)))
                        ps = bank(("y", e - 1))
                        pe.wait_ge(a_h1.sem, a_h1.at(i, 2 * e))
                        for t in range(NT):
                            for f in range(NF):
                                ins = product(ps[:, TOK[t]], h1[:, (e - 1) % 2, f, TOK[t]], W2[:, e - 1, f, :],
                                              f == 0, f == NF - 1)
                        ins.then_inc(full(("y", e - 1)), 1)

            gdn(0)
            ffn(0)
            if B > 1:
                with pe.Fori(1, B) as i:
                    gdn(i)
                    ffn(i)

        @block.vector
        def _(dve):
            v = nc.vector
            dve.wait_ge(loaded, 16 * len(loads))
            v.tensor_tensor(gate_bias[:, H:2 * H], gate_bias[:, H:2 * H], dt_bias[:], ALU.add).then_inc(vec_consts, 1)
            dve.wait_ge(vec_consts, 1)
            dve.wait_ge(pool_consts, 8)
            dve.wait_ge(act_consts, 6)

            def layer_norm(i, x_, st, mv_, rs, out_, sig, k, rsig, rk):
                for t in range(NT):
                    ins = v.bn_stats(st[:, t, :], x_[:, t, :])
                ins.then_inc(sig.sem, 1)
                dve.wait_ge(sig.sem, sig.at(i, k + 1))
                carry_waits(dve)
                for t in range(NT):
                    ins = v.bn_aggr(mv_[:, t, :], st[:, t, :])
                ins.then_inc(sig.sem, 1)
                dve.wait_ge(sig.sem, sig.at(i, k + 2))
                v.tensor_scalar(mv_[:, :, 1], mv_[:, :, 1], EPS_LN, None, ALU.add).then_inc(sig.sem, 1)
                dve.wait_ge(rsig.sem, rsig.at(i, rk))
                for t in range(NT):
                    v.tensor_scalar(out_[:, t, :], x_[:, t, :], mv_[:, t, 0:1], rs[:, t:t + 1], ALU.subtract,
                                    ALU.mult).then_inc(sig.sem, 1)

            def conv(i, n):
                use = ("qk", n) if n < NC else ("v", n - NC)
                which = ((0, n), (1, n)) if n < NC else ((2, 2 * (n - NC)), (2, 2 * (n - NC) + 1))
                dve.wait_ge(*full_at(i, use))
                ps = pair(bank(use))
                dve.wait_ge(a_acc.sem, a_acc.at(i, n + 1))
                for j in range(1, KT):
                    for m, (kind, c) in enumerate(which):
                        if j > 1:
                            dve.wait_ge(v_conv.sem, v_conv.at(i, 6 * n + 2 * (j - 2) + m + 1))
                        v.scalar_tensor_tensor(acc[:, n % 2, m, j:T], ps[:, m, 0:T - j],
                                               conv_w[:, kind, c, PAD - j:KT - j], acc[:, n % 2, m, j:T],
                                               ALU.mult, ALU.add).then_inc(v_conv.sem, 1)

            def gate(i):
                dve.wait_ge(a_gate.sem, a_gate.at(i, 2))
                v.tensor_scalar(den[:, :, 0:H], eabs[:, :, 0:H], 1.0, None, ALU.add).then_inc(v_gate.sem, 1)
                v.tensor_scalar(den[:, :, H:2 * H], eabs[:, :, H:2 * H], 2.0, None, ALU.add).then_inc(v_gate.sem, 1)
                dve.wait_ge(v_gate.sem, v_gate.at(i, 5))
                v.reciprocal(den[:], den[:]).then_inc(v_gate.sem, 1)
                dve.wait_ge(v_gate.sem, v_gate.at(i, 6))
                v.tensor_tensor(beta[:], emin[:], den[:, :, 0:H], ALU.mult).then_inc(v_gate.sem, 1)
                v.tensor_tensor(lp[:], eabs[:, :, H:2 * H], den[:, :, H:2 * H], ALU.mult).then_inc(v_gate.sem, 1)
                dve.wait_ge(v_gate.sem, v_gate.at(i, 8))
                v.tensor_tensor(lp2[:], lp[:], lp[:], ALU.mult).then_inc(v_gate.sem, 1)
                dve.wait_ge(v_gate.sem, v_gate.at(i, 9))
                v.tensor_scalar(lpp[:], lp2[:], 1.0 / 15, None, ALU.mult).then_inc(v_gate.sem, 1)
                for n, d in enumerate((13, 11, 9, 7, 5, 3)):
                    dve.wait_ge(v_gate.sem, v_gate.at(i, 10 + n))
                    v.scalar_tensor_tensor(lpp[:], lpp[:], 1.0 / d, lp2[:], ALU.add, ALU.mult)\
                        .then_inc(v_gate.sem, 1)
                dve.wait_ge(v_gate.sem, v_gate.at(i, 16))
                v.scalar_tensor_tensor(lpp[:], lpp[:], 1.0, lp[:], ALU.add, ALU.mult).then_inc(v_gate.sem, 1)
                v.tensor_scalar(lp2[:], z[:, :, H:2 * H], 0.0, 0.5, ALU.max, ALU.mult).then_inc(v_gate.sem, 1)
                dve.wait_ge(v_gate.sem, v_gate.at(i, 18))
                v.tensor_tensor(lpp[:], lpp[:], lp2[:], ALU.add).then_inc(v_gate.sem, 1)
                dve.wait_ge(v_gate.sem, v_gate.at(i, 19))
                v.scalar_tensor_tensor(lpp[:], lpp[:], 2.0, neg_A[:].unsqueeze(1).to_broadcast([P, NT, H]),
                                       ALU.mult, ALU.mult).then_inc(v_gate.sem, 1)

            def alpha_parts(i):
                dve.wait_ge(*full_at(i, "alphaT"))
                ps = bank("alphaT")
                a_t = ps[0:H, 0:T].rearrange("p (t k) -> p t k", t=NT)
                v.tensor_copy(al1[:], a_t).then_inc(v_alpha.sem, 1)
                dve.wait_ge(v_alpha.sem, v_alpha.at(i, 1))
                v.tensor_tensor(alr[:], a_t, al1[:], ALU.subtract).then_inc(v_alpha.sem, 1)
                dve.wait_ge(v_alpha.sem, v_alpha.at(i, 2))
                v.tensor_copy(al2[:], alr[:]).then_inc(v_alpha.sem, 1)
                v.tensor_copy(alpha3[0:H, :, 2:GW], al1[:, :, 1:P]).then_inc(v_alpha.sem, 1)
                dve.wait_ge(v_alpha.sem, v_alpha.at(i, 3))
                v.tensor_copy(alpha3[32:32 + H, :, 2:GW], al2[:, :, 1:P]).then_inc(v_alpha.sem, 1)
                v.tensor_tensor(alpha3[64:64 + H, :, 2:GW], alr[:, :, 1:P], al2[:, :, 1:P], ALU.subtract)\
                    .then_inc(v_alpha.sem, 1)
                v.tensor_tensor_scan(GT[:, 1:GW], ps[0:H, P:T], zeros[:], 1.0, ALU.mult, ALU.add)\
                    .then_inc(v_alpha.sem, 1)

            def gdn(i):
                dve.wait_ge(x_in.sem, x_in.at(i, 16))
                layer_norm(i, xin, stats, mv, rstd, xn, v_ln, 0, p_rstd, 1)
                dve.wait_ge(*full_at(i, "gate"))
                ps = bank("gate")
                v.tensor_tensor(z[:], ps[:, 0:NT * 2 * H].rearrange("p (t h) -> p t h", t=NT),
                                gate_bias[:].unsqueeze(1).to_broadcast([P, NT, 2 * H]), ALU.add)\
                    .then_inc(v_gate.sem, 1)
                dve.wait_ge(v_gate.sem, v_gate.at(i, 1))
                v.scalar_tensor_tensor(nabs[:], z[:], -1.0, z[:], ALU.mult, ALU.min).then_inc(v_gate.sem, 1)
                v.tensor_scalar(zmin[:], z[:, :, 0:H], 0.0, None, ALU.min).then_inc(v_gate.sem, 1)
                swap = [p ^ 1 for p in range(32)]
                for n in range(NCONV + 1):
                    if n < NCONV:
                        conv(i, n)
                    if n == 0:
                        gate(i)
                    if n == 2:
                        alpha_parts(i)
                    if n == 5:
                        dve.wait_ge(*full_at(i, "GT"))
                        ps = bank("GT")
                        v.tensor_copy(Gc[:].rearrange("p a h -> p (a h)"), ps[:, 0:2 * H]).then_inc(v_Gc.sem, 1)
                    if 1 <= n <= NC:
                        c = n - 1
                        dve.wait_ge(a_silu.sem, a_silu.at(i, c + 1))
                        if begun(i, c - 1):
                            dve.wait_ge(v_QK.sem, v_QK.at(i, c - 1))
                        carry_waits(dve)
                        v.stream_shuffle(rot[:, c % 2], qs[:, c % 2], swap).then_inc(v_rot.sem, 1)
                    if 2 <= n <= NC + 1:
                        c = n - 2
                        dve.wait_ge(p_rope.sem, p_rope.at(i, 2 * c + 2))
                        v.tensor_tensor(QK[:, c], qc[:, c % 2], rot[:, c % 2], ALU.add).then_inc(v_QK.sem, 1)
                dve.wait_ge(sums_done.sem, sums_done.at(i, NC))
                sums_ = bank("sums")[:, 0:NT * 3 * H].rearrange("p (t a h) -> p t a h", t=NT, a=3)
                v.tensor_scalar(sk[:, :, 0:2, :], sums_[:, :, 0:2, :], EPS_NORM, None, ALU.add).then_inc(v_sum.sem, 1)
                v.tensor_copy(sk[:, :, 2, :], sums_[:, :, 2, :]).then_inc(v_sum.sem, 1)
                dve.wait_ge(v_sum.sem, v_sum.at(i, 2))
                v.reciprocal(rk2[:], sk[:, :, 1, :]).then_inc(v_sum.sem, 1)
                dve.wait_ge(v_sum.sem, v_sum.at(i, 3))
                v.tensor_tensor(es[:], beta[:], rk2[:], ALU.mult).then_inc(v_sum.sem, 1)
                v.tensor_tensor(dd[:], sk[:, :, 2, :], rk2[:], ALU.mult).then_inc(v_sum.sem, 1)
                dve.wait_ge(v_sum.sem, v_sum.at(i, 5))
                v.tensor_tensor(dd[:], dd[:], D_bc[:].unsqueeze(1).to_broadcast([P, NT, H]), ALU.mult)\
                    .then_inc(v_sum.sem, 1)
                dve.wait_ge(p_nrm.sem, p_nrm.at(i, 1))
                for half in range(2):
                    for t in range(NT):
                        dve.wait_ge(*full_at(i, ("vT", t, half)))
                        ps = bank(("vT", t, half))
                        v.tensor_tensor(V[:, t, HALF[half], :], by_head(ps), bc(nrm[:, t, HALF[half]], DH), ALU.mult)\
                            .then_inc(v_V.sem, 1)
                for h in range(H + 1):
                    if h < H:
                        dve.wait_ge(*full_at(i, ("alpha", h)))
                        ps = bank(("alpha", h))
                        v.tensor_tensor_scan(Gam[:, h, :], ps[:, 0:NT * GW], ident_pad[:], 0.0, ALU.mult, ALU.add)\
                            .then_inc(v_Gam.sem, 1)
                    if h >= 1:
                        dve.wait_ge(*full_at(i, ("kk", h - 1)))
                        ps = bank(("kk", h - 1))
                        dve.wait_ge(v_Gam.sem, v_Gam.at(i, h))
                        for t in range(NT):
                            both = bass.AP(Gam[:].tensor, (h - 1) * NT * GW + t * GW, [[H * NT * GW, P], [1, 2], [1, P]])
                            ins = v.scalar_tensor_tensor(
                                NP[:, t * H + h - 1, :, :], ps[:, t * T:(t + 1) * T].rearrange("p (a k) -> p a k", a=2),
                                es[:, t, h - 1:h], both, ALU.mult, ALU.mult)
                        ins.then_inc(v_NP.sem, 1)
                v.tensor_tensor(fac[:], es[:, 0, :], Gam[:, :, P], ALU.mult).then_inc(v_Kt.sem, 1)
                dve.wait_ge(v_Kt.sem, v_Kt.at(i, 1))
                for half in range(2):
                    dve.wait_ge(*full_at(i, ("kT", half)))
                    ps = bank(("kT", half))
                    v.tensor_tensor(Kt[:, HALF[half], :], by_head(ps), bc(fac[:, HALF[half]], DH), ALU.mult)\
                        .then_inc(v_Kt.sem, 1)
                dve.wait_ge(a_diag.sem, a_diag.at(i, 2))
                dve.wait_ge(p_blk.sem, p_blk.at(i, 4))
                v.transpose(Eb[:], Dg[:]).then_inc(v_blk.sem, 1)
                
                for r in range(SB - 1):
                    n, w = SB - 1 - r, r + 1
                    dve.wait_ge(v_blk.sem, v_blk.at(i, 1 + 2 * r))
                    tmp_ = tmpb[:, 0:n * w].rearrange("p (a b) -> p a b", a=n)
                    v.tensor_tensor(tmp_, Eb[:, r + 1:, r:r + 1].to_broadcast([P, n, w]),
                                    X[:, r:r + 1, 0:w].to_broadcast([P, n, w]), ALU.mult).then_inc(v_blk.sem, 1)
                    dve.wait_ge(v_blk.sem, v_blk.at(i, 2 + 2 * r))
                    v.tensor_tensor(X[:, r + 1:, 0:w], X[:, r + 1:, 0:w], tmp_, ALU.subtract).then_inc(v_blk.sem, 1)
                dve.wait_ge(v_blk.sem, v_blk.at(i, 1 + 2 * (SB - 1)))
                v.transpose(XB[:], X[:].rearrange("p t c -> p c t")).then_inc(v_blk.sem, 1)
                for q in range(4):
                    off = SB * (q % 2)
                    v.transpose(Z[ROWS[q], :, off:off + SB].rearrange("p u t -> p t u"), X[ROWS[q]])\
                        .then_inc(v_blk.sem, 1)
                low = slice(DH, P)
                for t in range(NT):
                    right = V[:, 0] if t == 0 else R[:]
                    for half in range(2):
                        dve.wait_ge(*full_at(i, ("cross", t, half)))
                        ps = bank(("cross", t, half))
                        if t:
                            dve.wait_ge(p_R1.sem, p_R1.at(i, 2))
                        v.tensor_tensor(R[low, HALF[half], :], right[low, HALF[half], :], by_head(ps)[low],
                                        ALU.subtract).then_inc(v_R.sem, 1)
                    if t == 0:
                        for half in range(2):
                            dve.wait_ge(*full_at(i, ("KS", half)))
                            ps = bank(("KS", half))
                            v.tensor_tensor(R[:, PARITY[half], :], by_head(ps), bc(Gc[:, 0, PARITY[half]], DH), ALU.mult)\
                                .then_inc(v_R.sem, 1)
                        for half in range(2):
                            dve.wait_ge(*full_at(i, ("QS", half)))
                            ps = bank(("QS", half))
                            v.tensor_tensor(Kt[:, PARITY[half], :], by_head(ps), bc(Gc[:, 1, PARITY[half]], DH), ALU.mult)\
                                .then_inc(v_QS.sem, 1)
                    for half in range(2):
                        dve.wait_ge(*full_at(i, ("o", t, half)))
                        ps = bank(("o", t, half))
                        dve.wait_ge(p_Dv.sem, p_Dv.at(i, 1 if t == 0 else 4))
                        v.tensor_tensor(O[:, t, HALF[half], :], by_head(ps), Dv[:, HALF[half], :], ALU.add)\
                            .then_inc(v_O.sem, 1)
                dve.wait_ge(a_osq.sem, a_osq.at(i, 1))
                v.tensor_reduce(ms[:], V[:], AX.X, ALU.add).then_inc(v_ms.sem, 1)
                dve.wait_ge(v_ms.sem, v_ms.at(i, 1))
                v.scalar_tensor_tensor(ms[:], sk[:, :, 0, :], DH * EPS_NORM, ms[:], ALU.mult, ALU.add)\
                    .then_inc(v_ms.sem, 1)
                dve.wait_ge(v_ms.sem, v_ms.at(i, 2))
                v.tensor_scalar(ms[:], ms[:], 1.0 / DH, None, ALU.mult).then_inc(v_ms.sem, 1)
                for t in range(NT):
                    dve.wait_ge(a_sg.sem, a_sg.at(i, t + 1))
                    for half in range(2):
                        dve.wait_ge(*full_at(i, ("g", t, half)))
                        ps = bank(("g", t, half))
                        v.tensor_tensor(O[:, t, HALF[half], :], by_head(ps), O[:, t, HALF[half], :], ALU.mult)\
                            .then_inc(v_y.sem, 1)
                dve.wait_ge(*full_at(i, "Wo"))
                ps = bank("Wo")
                v.tensor_tensor(x1[:].rearrange("p t d -> p (t d)"), ps[:, 0:T], xin[:].rearrange("p t d -> p (t d)"),
                                ALU.add).then_inc(x1_ready.sem, 1)

            def ffn(i):
                dve.wait_ge(x1_ready.sem, x1_ready.at(i, 1))
                layer_norm(i, x1, fstats, fmv, frstd, xf, f_ln, 0, fp_rstd, 1)
                dve.wait_ge(f_ln.sem, f_ln.at(i, 5))
                layer_norm(i, xf, fstats, fmv, frstd, hn, f_ln, 5, fp_rstd, 2)
                dve.wait_ge(*full_at(i, "fqk"))
                ps = pair(bank("fqk"))
                v.tensor_copy(part[:, 0], ps).then_inc(v_part.sem, 1)
                dve.wait_ge(v_part.sem, v_part.at(i, 1))
                v.tensor_tensor(prest[:], ps, part[:, 0], ALU.subtract).then_inc(v_part.sem, 1)
                dve.wait_ge(v_part.sem, v_part.at(i, 2))
                v.tensor_copy(part[:, 1], prest[:]).then_inc(v_part.sem, 1)
                dve.wait_ge(v_part.sem, v_part.at(i, 3))
                v.tensor_tensor(part[:, 2], prest[:], part[:, 1], ALU.subtract).then_inc(v_part.sem, 1)
                dve.wait_ge(*full_at(i, "fv"))
                ps = bank("fv")
                v.tensor_copy(v9[:, :, :, 0:FD], ps[:, 0:T].rearrange("p (t h d) -> p t h d", t=NT, h=FH))\
                    .then_inc(v_v9.sem, 1)
                for h in range(FH):
                    dve.wait_ge(*full_at(i, ("max", h)))
                    ps = pair(bank(("max", h)))
                    v.tensor_reduce(mx[:, :, h], ps, AX.X, ALU.max).then_inc(v_mx.sem, 1)
                dve.wait_ge(v_mx.sem, v_mx.at(i, FH))
                v.tensor_scalar(mpart[:, 0], mx[:], -1.0, None, ALU.mult).then_inc(v_mp.sem, 1)
                dve.wait_ge(v_mp.sem, v_mp.at(i, 1))
                v.scalar_tensor_tensor(mrest[:], mx[:], -1.0, mpart[:, 0], ALU.mult, ALU.subtract)\
                    .then_inc(v_mp.sem, 1)
                dve.wait_ge(v_mp.sem, v_mp.at(i, 2))
                v.tensor_copy(mpart[:, 1], mrest[:]).then_inc(v_mp.sem, 1)
                dve.wait_ge(v_mp.sem, v_mp.at(i, 3))
                v.tensor_tensor(mpart[:, 2], mrest[:], mpart[:, 1], ALU.subtract).then_inc(v_mp.sem, 1)
                dve.wait_ge(v_mp.sem, v_mp.at(i, 4))
                v.tensor_copy(mpad[:, :, :, ROW6:ROW6 + NS], mpart[:].rearrange("p s t h -> p t h s"))\
                    .then_inc(v_mp.sem, 1)
                for m in range(NC // 2):
                    dve.wait_ge(*full_at(i, ("mrow", m)))
                    ps = pair(bank(("mrow", m)))
                    v.tensor_tensor(QK6[:, 2 * m:2 * m + 2, 0, :], QK6[:, 2 * m:2 * m + 2, 0, :], ps, ALU.add)\
                        .then_inc(v_mrow.sem, 1)
                dve.wait_ge(pv_done.sem, pv_done.at(i, FH))
                pv = bank("pv")[:, 0:NT * FH * (FD + 1)].rearrange("p (t h d) -> p t h d", t=NT, h=FH)
                v.reciprocal(rec[:], pv[:, :, :, FD]).then_inc(v_ctx.sem, 1)
                dve.wait_ge(v_ctx.sem, v_ctx.at(i, 1))
                v.tensor_tensor(ctxn[:].rearrange("p t (h d) -> p t h d", h=FH), pv[:, :, :, 0:FD], bc(rec[:], FD),
                                ALU.mult).then_inc(v_ctx.sem, 1)
                dve.wait_ge(*full_at(i, "fWo"))
                ps = bank("fWo")
                v.tensor_tensor(x2[:].rearrange("p t d -> p (t d)"), ps[:, 0:T], xf[:].rearrange("p t d -> p (t d)"),
                                ALU.add).then_inc(v_x2.sem, 1)
                dve.wait_ge(v_x2.sem, v_x2.at(i, 1))
                layer_norm(i, x2, fstats, fmv, frstd, hn, f_ln, 10, fp_rstd, 3)
                dve.wait_ge(*full_at(i, "router"))
                ps = bank("router")
                l_ = ps[:, 0:NT * NE].rearrange("p (t e) -> p t e", t=NT)
                v.tensor_reduce(lmax[:], l_, AX.X, ALU.max).then_inc(v_lg.sem, 1)
                dve.wait_ge(v_lg.sem, v_lg.at(i, 1))
                v.tensor_tensor(lg[:], l_, bc(lmax[:], NE), ALU.subtract).then_inc(v_lg.sem, 1)
                dve.wait_ge(a_ex.sem, a_ex.at(i, 1))
                mine = ex[:].unsqueeze(3).to_broadcast([P, NT, NE, NE])
                other = ex[:].unsqueeze(2).to_broadcast([P, NT, NE, NE])
                v.tensor_tensor(gt[:], other, mine, ALU.is_gt).then_inc(v_w.sem, 1)
                v.tensor_tensor(eq[:], other, mine, ALU.is_equal).then_inc(v_w.sem, 1)
                dve.wait_ge(v_w.sem, v_w.at(i, 2))
                v.tensor_tensor(eq[:], eq[:], earlier[:].rearrange("p (a b) -> p a b", a=NE).unsqueeze(1)
                                .to_broadcast([P, NT, NE, NE]), ALU.mult).then_inc(v_w.sem, 1)
                dve.wait_ge(v_w.sem, v_w.at(i, 3))
                v.tensor_tensor(gt[:], gt[:], eq[:], ALU.add).then_inc(v_w.sem, 1)
                dve.wait_ge(v_w.sem, v_w.at(i, 4))
                v.tensor_reduce(rank[:], gt[:], AX.X, ALU.add).then_inc(v_w.sem, 1)
                dve.wait_ge(v_w.sem, v_w.at(i, 5))
                v.scalar_tensor_tensor(wsel[:], rank[:], 2.0, ex[:], ALU.is_lt, ALU.mult).then_inc(v_w.sem, 1)
                dve.wait_ge(v_w.sem, v_w.at(i, 6))
                v.tensor_reduce(wden[:], wsel[:], AX.X, ALU.add).then_inc(v_w.sem, 1)
                dve.wait_ge(v_w.sem, v_w.at(i, 7))
                v.reciprocal(wden[:], wden[:]).then_inc(v_w.sem, 1)
                dve.wait_ge(v_w.sem, v_w.at(i, 8))
                v.tensor_tensor(wsel[:], wsel[:], bc(wden[:], NE), ALU.mult).then_inc(v_w.sem, 1)
                dve.wait_ge(*full_at(i, "wT"))
                ps = bank("wT")
                v.tensor_copy(wT[:], ps[0:NE, 0:T]).then_inc(v_wT.sem, 1)
                dve.wait_ge(*full_at(i, "b2"))
                ps = bank("b2")
                dve.wait_ge(p_xs.sem, p_xs.at(i, 1))
                if not (isinstance(i, int) and i == 0):
                    dve.wait_ge(out_stored.sem, out_stored.at(i, 0))
                v.tensor_tensor(moe[:].rearrange("p t d -> p (t d)"), ps[:, 0:T], x1[:].rearrange("p t d -> p (t d)"),
                                ALU.add).then_inc(v_moe.sem, 1)
                for e in range(NE):
                    dve.wait_ge(*full_at(i, ("y", e)))
                    ps = bank(("y", e))
                    dve.wait_ge(v_moe.sem, v_moe.at(i, e + 1))
                    for t in range(NT):
                        ins = v.scalar_tensor_tensor(moe[:, t, :], ps[:, TOK[t]], wsel[:, t, e:e + 1], moe[:, t, :],
                                                     ALU.mult, ALU.add)
                    ins.then_inc(v_moe.sem, 1)

            gdn(0)
            ffn(0)
            if B > 1:
                with dve.Fori(1, B) as i:
                    gdn(i)
                    ffn(i)


def tables():
    c = {"c_ident": np.eye(P)}
    pad = np.zeros((P, NT, GW))
    pad[:, :, 1:] = np.eye(P)[:, None, :]
    c["c_ident_pad"] = pad.reshape(P, -1)
    inv = (1.0 / np.float32(10000.0) ** (np.arange(0, DH, 2, dtype=np.float32) / np.float32(DH))).astype(np.float32)
    freqs = np.outer(np.arange(T, dtype=np.float32), inv).astype(np.float32)
    emb = np.concatenate([freqs, freqs], -1)[:, ::2]
    rows = np.arange(P) % DH // 2
    sign = np.where(np.arange(P) % 2 == 0, -1.0, 1.0)[:, None]
    c["c_cos"] = np.cos(emb)[:, rows].T
    c["c_sin"] = np.sin(emb)[:, rows].T * sign
    c["c_head_rows"] = (np.arange(P)[:, None] // DH == np.arange(2)[None, :])
    sel = np.zeros((P, H, P))
    for h in range(H):
        sel[[h, 32 + h, 64 + h], h, :] = 1.0
    c["c_alpha_sel"] = sel.reshape(P, -1)
    for name, split in (("c_q_sel", SPLIT_Q), ("c_k_sel", SPLIT_K)):
        sel = np.zeros((P, NS, NC, P))
        for h in range(FH):
            for n, s in enumerate(split):
                for d in range(FD):
                    sel[h * FD + d, s, h // 2, (h % 2) * DH + n * FD + d] = 1.0
        c[name] = sel.reshape(P, -1)
    r = np.arange(P) % DH
    c["c_k_ones"] = ((r >= ROW6) & (r < ROW6 + NS))[:, None]
    c["c_earlier"] = np.tile((np.arange(NE)[None, :] < np.arange(NE)[:, None]).reshape(1, -1), (P, 1))
    return {k: np.ascontiguousarray(x, dtype=np.float32) for k, x in c.items()}


def kernel(**inputs):
    import concourse.bacc as bacc
    from concourse.bass_utils import run_bass_kernel_spmd

    x = {k: np.asarray(a) for k, a in inputs.items()}
    att = {k[len("L0_attn_"):]: a for k, a in x.items() if k.startswith("L0_attn_")}
    ffn = {k[len("L0_ffn_"):]: a for k, a in x.items() if k.startswith("L0_ffn_")}
    arrays = {k: att[k] for k in ("x", "Wq", "Wk", "Wv", "Wg", "Wo", "bw", "bb", "gkw", "gkb", "dt_bias", "A_log",
                                  "D_param", "onorm_w")}
    arrays["conv_w"] = np.stack([att[k][:, 0, :].reshape(NC, P, KT).transpose(1, 0, 2) for k in ("qcw", "kcw", "vcw")], 1)
    arrays["conv_b"] = np.stack([att[k].reshape(NC, P).T for k in ("qcb", "kcb", "vcb")], 1)
    for k in ("Wq", "Wk", "Wv", "Wo", "Wg"):
        arrays["f" + k] = ffn[k]
    for k in ("ln1_g", "ln1_b", "ln2_g", "ln2_b"):
        arrays[k] = ffn[k].reshape(HID, 1)
    arrays["W1"], arrays["W2"], arrays["b2"] = ffn["W1"], ffn["W2"], ffn["b2"]
    arrays["b1"] = ffn["b1"].reshape(NE, NF, P).transpose(2, 0, 1)
    arrays.update(tables())

    nc = bacc.Bacc("TRN2", target_bir_lowering=False, num_devices=1)
    feed, args = {}, {}
    for k, v in arrays.items():
        v = np.ascontiguousarray(v)
        feed[f"in_{k}"] = v
        args[k] = nc.dram_tensor(f"in_{k}", v.shape, mybir.dt.from_np(v.dtype), kind="ExternalInput").ap()
    out = nc.dram_tensor("out", x["L0_attn_x"].shape, F32, kind="ExternalOutput").ap()
    program(nc, args, out)
    r = run_bass_kernel_spmd(nc, [feed], core_ids=[0])
    return r.results[0]["out"]
```

```python
from contextlib import ExitStack

import numpy as np
import concourse.bass as bass
from concourse import mybir

F32 = mybir.dt.float32
BF16 = mybir.dt.bfloat16
ALU = mybir.AluOpType
ACT = mybir.ActivationFunctionType
AX = mybir.AxisListType

P = 128
T = 256
NT = T // P
HID = 128
H = 16
DH = 64
CH = H * DH
NC = CH // P
KT = 4
PAD = KT - 1
NU = NT * H
FH = 16
FD = HID // FH
NE = 8
FF = 512
NF = FF // P
SB = 32
SPLIT = 8
GW = P + 1
EPS_NORM = 1e-6
EPS_LN = 1e-5
NCONV = 3 * NC // 2
SUMS_LAG = 2
NS = 3
ROW6 = 6 * FD
SPLIT_Q = (0, 0, 1, 0, 2, 1)
SPLIT_K = (0, 1, 0, 2, 0, 1)


class Signal:

    def __init__(self, sem, per):
        self.sem, self.per = sem, per

    def at(self, i, k):
        if isinstance(i, tuple):
            return i[0] * self.per + (k - i[1] * self.per)
        return i * self.per + k


def bank_uses():
    g = [("xT", 0, "xnT_ready", 1), ("gate", 1, "v_gate", 1)]
    g += [(("qk", c), c % 4, "v_conv", 6 * (c + 1)) for c in range(4)]
    g += [("alphaT", 1, "v_alpha", 7), ("GT", 2, "v_Gc", 1), ("sums", 4, "v_sum", 2)]
    g += [(("qk", c), c % 4, "v_conv", 6 * (c + 1)) for c in range(4, NC)]
    g += [(("v", m), m % 2, "v_conv", 6 * (NC + m + 1)) for m in range(4)]
    g += [(("vT", t, half), 2 + t, "a_V", 2 * half + t + 1) for half in range(2) for t in range(NT)]
    for h in range(H):
        g += [(("alpha", h), h % 2, "v_Gam", h + 1), (("kk", h), 2 + h % 2, "v_NP", h + 1)]
    g += [(("kT", half), half, "v_Kt", 5 + half) for half in range(2)]
    g += [(("join1", half), 2 + half, "a_T1", half + 1) for half in range(2)]
    g += [(("join2", half), half, "a_Z", 2) for half in range(2)]
    for t in range(NT):
        for half in range(2):
            if t:
                g += [(("QS", half), 2 + 2 * half, "v_QS", half + 1)]
            g += [(("top", t, half), half, "a_W", 4 * t + half + 1),
                  (("cross", t, half), 2 + half, "v_R", 4 * t + half + 1),
                  (("low", t, half), half, "a_W", 4 * t + half + 3)]
        if not t:
            g += [("S", 4, "a_S", 1)]
            for half in range(2):
                g += [(("KS", half), 2 + half, "v_R", 3 + half)]
        g += [(("o", t, half), 2 + half, "v_O", 2 * t + half + 1) for half in range(2)]
    g += [(("g", t, half), 2 * t + half, "a_g", 2 * t + half + 1) for t in range(NT) for half in range(2)]
    f = [(("yT", t, half), 5 + (2 * t + half) % 3, "a_yT", 2 * t + half + 1) for t in range(NT) for half in range(2)]
    f += [("Wo", 6, "x1_ready", 1), ("hT", 7, "a_hT", 1), ("fqk", 5, "v_part", 2), ("fv", 6, "v_v9", 1)]
    f += [(("rep", c), 5 + (c + 2) % 3, "a_QK6", 2 * c + 2) for c in range(NC)]
    f += [(("max", h), 5 + h % 3, "v_mx", h + 1) for h in range(FH)]
    f += [(("mrow", c), 5 + c % 3, "v_mrow", 1 if c == 0 else NC // 2) for c in range(NC // 2)]
    f += [(("st", h), 5 + h % 2, "a_pT", h + 1) for h in range(FH)]
    f += [(("pv", half), 7, "a_ctx9", half + 1) for half in range(2)]
    f += [(("ctx", t), 5 + t, "v_ctx", 2 * t + 2) for t in range(NT)]
    f += [("ctxT", 7, "a_ctxT", 1), ("fWo", 5, "v_x2", 1), ("mT", 6, "a_hT", 2), ("router", 7, "v_lg", 2),
          ("wT", 5, "v_wT", 1), ("b2", 6, "v_moe", 1)]
    for e in range(NE):
        f += [(("h1", e, 0), 5, "a_h1", 2 * e + 1), (("h1", e, 1), 6, "a_h1", 2 * e + 2),
              (("y", e), 7, "v_moe", e + 2)]
    return g + f


FFN_STEPS = ([(step, 0) for step in ("norm", "silu", "y")] + [("yT", t) for t in range(NT)]
             + [(step, 0) for step in ("Wo", "ln", "hT", "fqk", "fv")] + [("rep", c) for c in range(NC)]
             + [("max", h) for h in range(FH)] + [("mrow", m) for m in range(NC // 2)]
             + [("att", h) for h in range(FH + 1)]
             + [("ctx", t) for t in range(NT)] + [(step, 0) for step in ("ctxT", "fWo", "mT", "router", "wT", "b2")]
             + [("up", 0)] + [x for e in range(1, NE) for x in (("up", e), ("down", e - 1))] + [("down", NE - 1)])

BESIDE = {
    ("conv", 0): ("y", 0), ("conv", 3): ("yT", 1), ("conv", 5): ("Wo", 0), ("conv", 8): ("ln", 0),
    ("conv", 10): ("hT", 0), ("conv", 12): ("fqk", 0), ("head", 1): ("rep", 1), ("head", 2): ("rep", 1),
    ("head", 3): ("rep", 2), ("head", 6): ("rep", 2), ("head", 10): ("rep", 2), ("head", 13): ("rep", 3),
    ("head", 14): ("rep", 3), ("head", 15): ("rep", 3), "kT": ("rep", 3), ("block", 2): ("rep", 4),
    ("block", 3): ("att", 0), ("block", 11): ("att", 3), ("block", 13): ("att", 4), ("block", 15): ("att", 5),
    ("block", 16): ("att", 12), ("block", 21): ("att", 14), ("block", 23): ("att", 15), ("block", 29): ("ctx", 1),
    ("block", SB - 2): ("ctxT", 0), "join": ("fWo", 0), ("top", 0): ("mT", 0), ("cross", 0): ("up", 1),
    ("low", 0): ("down", 0), "S": ("down", 1), ("o", 0): ("up", 4), ("top", 1): ("down", 3),
    ("cross", 1): ("down", 4), ("low", 1): ("down", 4), ("o", 1): ("down", 7),
}


def beside(ffn, j):
    taken = [0]

    def upto(milestone):
        if milestone is None or milestone in BESIDE:
            end = len(FFN_STEPS) if milestone is None else FFN_STEPS.index(BESIDE[milestone]) + 1
            for step, n in FFN_STEPS[taken[0]:end]:
                ffn(j, step, n)
            taken[0] = max(taken[0], end)
    return upto


def alone(milestone):
    pass


OWN_SIGNAL = {("pv", 0), ("pv", 1)}


def program(nc, a, out):
    B = a["x"].shape[0]
    table = bank_uses()
    signals = {}

    with ExitStack() as ctx:
        def sb(name, shape, dt=F32):
            return ctx.enter_context(nc.sbuf_tensor(name, shape, dt))

        def signal(name, per):
            signals[name] = Signal(ctx.enter_context(nc.semaphore(name)), per)
            return signals[name]

        def sem(name):
            return ctx.enter_context(nc.semaphore(name))

        banks = [ctx.enter_context(nc.psum_tensor(f"bank{b}", [P, 512], F32)) for b in range(8)]
        bank_full = [sem(f"bank{b}_full") for b in range(8)]
        bank_of = {use: b for use, b, _, _ in table}
        filled, full_per, before, last_of = {}, [0] * 8, {}, {}
        for use, b, name, k in table:
            before[use] = last_of.get(b)
            last_of[b] = (name, k)
            if use not in OWN_SIGNAL:
                full_per[b] += 1
                filled[use] = full_per[b]
        for use, b, _, _ in table:
            if before[use] is None:
                before[use] = (last_of[b][0], last_of[b][1] - 10 ** 6)

        def begun(i, k):
            return k > 0 or not (isinstance(i, int) and i == 0)

        def carry_waits(eng):
            eng.sem_inc(passed, 1)

        def bank(use):
            return banks[bank_of[use]]

        def full_at(i, use):
            return bank_full[bank_of[use]], Signal(None, full_per[bank_of[use]]).at(i, filled[use])

        def emptied(use):
            name, k = before[use]
            return signals[name], k + 10 ** 6 - signals[name].per if k < 0 else k

        def reused(i, use):
            return begun(i, emptied(use)[1])

        def free_at(i, use):
            sig, k = emptied(use)
            return sig.sem, sig.at(i, k)

        def full(use):
            return bank_full[bank_of[use]]

        ident = sb("ident", [P, P])
        identb = sb("identb", [P, P], BF16)
        ident_pad = sb("ident_pad", [P, NT * GW])
        cos = sb("cos", [P, T])
        sin = sb("sin", [P, T])
        head_cols = sb("head_cols", [P, 2 * (H - 1) + 16])
        alpha_sel = sb("alpha_sel", [P, H * P], BF16)
        q_sel = sb("q_sel", [P, NS, NC, P], BF16)
        k_sel = sb("k_sel", [P, NS, NC, P], BF16)
        k_ones = sb("k_ones", [P, 1])
        earlier = sb("earlier", [P, NE * NE])
        Wqkv = sb("Wqkv", [P, 3, CH])
        Wg = sb("Wg", [P, CH])
        Wo = sb("Wo", [P, NC, HID])
        conv_w = sb("conv_w", [P, 3, NC, KT])
        conv_b = sb("conv_b", [P, 3, NC])
        Wgate = sb("Wgate", [P, 2 * H])
        gate_bias = sb("gate_bias", [P, 2 * H])
        dt_bias = sb("dt_bias", [P, H])
        neg_A = sb("neg_A", [P, H])
        A_log = sb("A_log", [P, H])
        D_bc = sb("D_bc", [P, H])
        onorm = sb("onorm", [P, DH])
        fW = sb("fW", [P, 4, HID])
        ln_gb = sb("ln_gb", [P, 4])
        Wr = sb("Wr", [P, NE])
        W1 = sb("W1", [P, NE, FF])
        b1 = sb("b1", [P, NE, NF])
        W2 = sb("W2", [P, NE, NF, HID])
        b2 = sb("b2", [NE, HID])
        neg_half = sb("neg_half", [P, 1])
        half_c = sb("half_c", [P, 1])
        zeros = sb("zeros", [H, P])

        xin = sb("xin", [P, NT, HID])
        stats = sb("stats", [P, NT, 6])
        mv = sb("mv", [P, NT, 2])
        rstd = sb("rstd", [P, NT])
        xn = sb("xn", [P, NT, HID])
        xnT = sb("xnT", [P, T])
        z = sb("z", [P, NT, 2 * H])
        nabs = sb("nabs", [P, NT, 2 * H])
        zmin = sb("zmin", [P, NT, H])
        eabs = sb("eabs", [P, NT, 2 * H])
        emin = sb("emin", [P, NT, H])
        den = sb("den", [P, NT, 2 * H])
        beta = sb("beta", [P, NT, H])
        lp = sb("lp", [P, NT, H])
        lp2 = sb("lp2", [P, NT, H])
        lpp = sb("lpp", [P, NT, H])
        alpha = sb("alpha", [P, NT, H])
        al1 = sb("al1", [H, NT, P], BF16)
        alr = sb("alr", [H, NT, P])
        al2 = sb("al2", [H, NT, P], BF16)
        alpha3 = sb("alpha3", [P, NT, GW], BF16)
        GT = sb("GT", [H, GW])
        Gc = sb("Gc", [P, 2, H])
        QK = sb("QK", [P, NC, 2, T])
        sk = sb("sk", [P, NT, 3, H])
        rk2 = sb("rk2", [P, NT, H])
        nrm = sb("nrm", [P, NT, H])
        es = sb("es", [P, NT, H])
        dd = sb("dd", [P, NT, H])
        fac = sb("fac", [P, H])
        V = sb("V", [P, NT, H, DH])
        Gam = sb("Gam", [P, H, NT * GW])
        NP = sb("NP", [P, NU, 2, P])
        tmpb = sb("tmpb", [P, SB * SB // 4])
        Z = sb("Z", [P, NU, 2 * SB])
        Kt = sb("Kt", [P, H, DH])
        S = sb("S", [P, NC, DH])
        ms = sb("ms", [P, NT, H])

        def over(tile, n, shape):
            letters = "abcd"[:len(tile.shape) - 1]
            flat = tile[:].rearrange(f"p {' '.join(letters)} -> p ({' '.join(letters)})")
            size = int(np.prod(shape))
            names = "uvw"[:len(shape)]
            return flat[:, 1024 * n:1024 * n + size].rearrange(
                f"p ({' '.join(names)}) -> p {' '.join(names)}", **dict(zip(names, shape)))

        Dg = over(Gam, 0, [SB, NU])
        Eb = over(Gam, 1, [SB, SB])
        X = over(Gam, 2, [SB, SB])
        XB = over(Gam, 3, [SB, NU])
        O = [over(Gam, 0, [H, DH]), over(Gam, 3, [H, DH])]
        yT = [over(Gam, 1, [NC, P]), over(Gam, 2, [NC, P])]
        T1 = over(Gam, 0, [NU, SB])
        tmpp = over(Gam, 0, [SB, SB])
        R = over(Gam, 1, [H, DH])
        W = [over(Gam, 2, [H, DH]), V[:, 0]]
        Dv = over(Gam, 3, [H, DH])
        acc = over(NP, 0, [2, 2, T])
        qs = over(NP, 1, [2, 2, T])
        rot = over(NP, 2, [2, 2, T])
        qc = over(NP, 3, [2, 2, T])
        vs = over(NP, 4, [NC, T])
        sq = over(NP, 6, [2, 3, T])
        sumsT = over(NP, 7, [3, T])[:, 2, :]
        squares = [over(NP, 0, [H, DH]), over(NP, 1, [H, DH])]
        fo = sb("fo", [P, NT, H])
        x1 = sb("x1", [P, NT, HID])

        fstats = sb("fstats", [P, NT, 6])
        fmv = sb("fmv", [P, NT, 2])
        frstd = sb("frstd", [P, NT])
        xf = sb("xf", [P, NT, HID])
        hn = sb("hn", [P, NT, HID])
        hT = sb("hT", [P, T])
        v9 = sb("v9", [P, NT * FH * (FD + 1) + 32])
        QK6 = sb("QK6", [P, NC, 2, T], BF16)
        mx = sb("mx", [P, NT, FH])
        mrest = sb("mrest", [P, NT, FH])
        mpart = sb("mpart", [P, NS, NT, FH], BF16)
        mpad = sb("mpad", [P, NT, FH, DH], BF16)
        pT = sb("pT", [P, 4, NT, T])
        part = pT[:, 2:4].rearrange("p a b t -> p (a b t)")[:, 0:NS * T].bitcast(BF16)\
            .rearrange("p (s a t) -> p s a t", s=NS, a=2)
        ctx9 = QK6[:, 0:4].rearrange("p c a t -> p (c a t)").bitcast(F32).rearrange("p (g t) -> p g t", g=4)
        prest = pT[:, 1]
        rec = sb("rec", [P, NT, FH])
        ctxn = sb("ctxn", [P, NT, HID])
        ctxT = hT
        x2 = sb("x2", [P, NT, HID])
        mT = sb("mT", [P, T])
        lg = sb("lg", [P, NT, NE])
        lmax = sb("lmax", [P, NT])
        ex = sb("ex", [P, NT, NE])
        gt = sb("gt", [P, NT, NE, NE])
        eq = sb("eq", [P, NT, NE, NE])
        rank = sb("rank", [P, NT, NE])
        wsel = sb("wsel", [P, NT, NE])
        wden = sb("wden", [P, NT])
        wT = sb("wT", [NE, T])
        h1 = QK6[:].bitcast(F32).rearrange("p (e f) a t -> p e f (a t)", e=2)
        moe = sb("moe", [P, NT, HID])

        def v9_tile():
            return v9[:, 0:NT * FH * (FD + 1)].rearrange("p (t h d) -> p t h d", t=NT, h=FH)

        loaded = sem("weights_loaded")
        loaded_ffn = sem("second_block_weights_loaded")
        pool_consts = sem("pool_constants_ready")
        act_consts = sem("act_constants_ready")
        vec_consts = sem("vector_constants_ready")
        passed = sem("waits_passed")
        x_in = Signal(sem("x_in"), 16)
        out_stored = Signal(sem("out_stored"), 16)
        x1_ready = signal("x1_ready", 1)
        v_ln = signal("v_ln", 5)
        p_rstd = signal("p_rstd", 1)
        xnT_ready = signal("xnT_ready", 1)
        v_gate = signal("v_gate", 20)
        a_gate = signal("a_gate", 3)
        v_alpha = signal("v_alpha", 7)
        v_Gc = signal("v_Gc", 1)
        a_acc = signal("a_acc", NCONV)
        v_conv = signal("v_conv", 6 * NCONV)
        a_silu = signal("a_silu", NCONV)
        v_rot = signal("v_rot", NC)
        p_sq = signal("p_sq", NC)
        sums_done = signal("sums_done", NC)
        p_rope = signal("p_rope", 2 * NC)
        v_QK = signal("v_QK", NC)
        v_sum = signal("v_sum", 6)
        p_nrm = signal("p_nrm", 1)
        a_V = signal("a_V", 4)
        p_V = signal("p_V", 2)
        v_Gam = signal("v_Gam", H)
        v_NP = signal("v_NP", H)
        a_diag = signal("a_diag", 4)
        p_blk = signal("p_blk", 2 + 2 * (SB - 1 - SPLIT))
        v_blk = signal("v_blk", 1 + 2 * (SB - 1) + 5)
        a_T1 = signal("a_T1", 2)
        a_Z = signal("a_Z", 2)
        v_Kt = signal("v_Kt", 6)
        a_W = signal("a_W", 8)
        v_R = signal("v_R", 6)
        a_S = signal("a_S", 1)
        p_R1 = signal("p_R1", 2)
        p_Dv = signal("p_Dv", 4)
        v_QS = signal("v_QS", 2)
        v_O = signal("v_O", 4)
        a_osq = signal("a_osq", NT)
        a_g = signal("a_g", 4)
        a_sq = signal("a_sq", NC)
        a_sums = signal("a_sums", 1)
        p_x1 = signal("p_x1", 1)
        v_ms = signal("v_ms", 3 * NT)
        p_f = signal("p_f", NT)
        p_on = signal("p_on", 4)
        a_sg = signal("a_sg", 2)
        v_y = signal("v_y", 2)
        a_yT = signal("a_yT", 4)
        f_ln = signal("f_ln", 15)
        fp_rstd = signal("fp_rstd", 3)
        a_hT = signal("a_hT", 2)
        v_part = signal("v_part", 4)
        v_v9 = signal("v_v9", 1)
        a_QK6 = signal("a_QK6", 2 * NC)
        v_mx = signal("v_mx", FH)
        v_mp = signal("v_mp", 5)
        v_mrow = signal("v_mrow", NC // 2)
        a_pT = signal("a_pT", FH)
        pv_done = signal("pv_done", 4)
        v_ctx = signal("v_ctx", 2 * NT)
        a_ctx9 = signal("a_ctx9", 2)
        a_ctxT = signal("a_ctxT", 1)
        v_x2 = signal("v_x2", 1)
        p_xs = signal("p_xs", 1)
        v_lg = signal("v_lg", 2)
        a_ex = signal("a_ex", 1)
        v_w = signal("v_w", 9)
        v_wT = signal("v_wT", 1)
        a_h1 = signal("a_h1", 2 * NE)
        v_moe = signal("v_moe", 1 + NE)

        def batches(eng, gdn, ffn, first=lambda: None):
            first()
            gdn(0, alone)
            eng.wait_ge(loaded_ffn, 16 * len(loads_ffn))
            if B > 1:
                gdn(1, beside(ffn, 0))
            if B > 2:
                with eng.Fori(2, B) as i:
                    gdn(i, beside(ffn, (i, 1)))
            beside(ffn, B - 1)(None)

        block = ctx.enter_context(nc.Block())

        stage = NP[:, :, :, :].rearrange("p u a b -> p (u a b)")
        n_q = NS * NC * P
        loads = [(ident[:], a["c_ident"]), (ident_pad[:], a["c_ident_pad"]), 
                 (cos[:], a["c_cos"]), (sin[:], a["c_sin"]), (head_cols[:], a["c_head_cols"]),
                 (k_ones[:], a["c_k_ones"]), (earlier[:], a["c_earlier"]),
                 (stage[:, 0:H * P], a["c_alpha_sel"]),
                 (stage[:, H * P:H * P + n_q], a["c_q_sel"]),
                 (stage[:, H * P + n_q:H * P + 2 * n_q], a["c_k_sel"]),
                 (Wqkv[:, 0, :], a["Wq"]), (Wqkv[:, 1, :], a["Wk"]), (Wqkv[:, 2, :], a["Wv"]),
                 (Wg[:], a["Wg"]), (Wo[:], a["Wo"].rearrange("(c p) n -> p c n", p=P)),
                 (conv_w[:], a["conv_w"]), (conv_b[:], a["conv_b"]),
                 (Wgate[:, 0:H], a["bw"]), (Wgate[:, H:2 * H], a["gkw"]),
                 (gate_bias[:, 0:H], a["bb"].partition_broadcast(P)),
                 (gate_bias[:, H:2 * H], a["gkb"].partition_broadcast(P)),
                 (dt_bias[:], a["dt_bias"].partition_broadcast(P)),
                 (A_log[:], a["A_log"].partition_broadcast(P)),
                 (D_bc[:], a["D_param"].partition_broadcast(P)),
                 (onorm[:], a["onorm_w"].partition_broadcast(P))]
        loads_ffn = [(fW[:, 0, :], a["fWq"]), (fW[:, 1, :], a["fWk"]), (fW[:, 2, :], a["fWv"]), (fW[:, 3, :], a["fWo"]),
                     (ln_gb[:, 0:1], a["ln1_g"]), (ln_gb[:, 1:2], a["ln1_b"]),
                     (ln_gb[:, 2:3], a["ln2_g"]), (ln_gb[:, 3:4], a["ln2_b"]),
                     (Wr[:], a["fWg"]), (W1[:], a["W1"].rearrange("e d f -> d e f")), (b1[:], a["b1"]),
                     (W2[:], a["W2"].rearrange("e (c p) d -> p e c d", p=P)), (b2[:], a["b2"])]

        def bc(ap, n):
            sh = list(ap.shape)
            return ap.unsqueeze(len(sh)).to_broadcast(sh + [n])

        def x_rows(i):
            return a["x"][bass.ds(i, 1)].rearrange("a (t p) d -> p (a t) d", p=P)

        def out_rows(i):
            return out[bass.ds(i, 1)].rearrange("a (t p) d -> p (a t) d", p=P)

        QUARTERS = (4, 8, 12, 16)
        HALF = [slice(0, 8), slice(8, 16)]
        PARITY = [slice(0, H, 2), slice(1, H, 2)]
        ROWS = [slice(SB * q, SB * q + SB) for q in range(P // SB)]
        TOK = [slice(t * P, t * P + P) for t in range(NT)]

        def rows_of(h):
            return slice((h % 2) * DH, (h % 2) * DH + DH)

        def pair(tile):
            return tile[:].rearrange("p (a t) -> p a t", a=2)

        def by_head(tile):
            return tile[:].rearrange("p (h d) -> p h d", h=8)

        def by_unit(tile):
            return tile[:].rearrange("p (u s) -> p u s", u=16)

        @block.sync
        def _(sp):
            for dst, src in loads:
                sp.dma_start(dst, src).then_inc(loaded, 16)
            sp.dma_start(xin[:], x_rows(0)).then_inc(x_in.sem, 16)
            sp.wait_ge(loaded, 16 * len(loads))
            for dst, src in loads_ffn:
                sp.dma_start(dst, src).then_inc(loaded_ffn, 16)

            def load(i, following):
                sp.wait_ge(p_x1.sem, p_x1.at(i, 1))
                sp.dma_start(xin[:], x_rows(following)).then_inc(x_in.sem, 16)

            def store(i, which):
                sp.wait_ge(v_moe.sem, v_moe.at(i, v_moe.per))
                sp.dma_start(out_rows(which), moe[:]).then_inc(out_stored.sem, 16)

            if B > 1:
                load(0, 1)
            if B > 2:
                with sp.Fori(1, B - 1) as i:
                    load(i, i + 1)
                    store((i, 1), i - 1)
            load(B - 1, B - 1)
            if B > 1:
                store(B - 2, B - 2)
            store(B - 1, B - 1)
            sp.wait_ge(out_stored.sem, out_stored.at(B, 0))

        @block.gpsimd
        def _(pool):
            g = nc.gpsimd
            g.memset(neg_half[:], -0.5).then_inc(pool_consts, 1)
            g.memset(half_c[:], 0.5).then_inc(pool_consts, 1)
            g.memset(alpha3[:], 0.0).then_inc(pool_consts, 1)
            g.memset(Z[:], 0.0).then_inc(pool_consts, 1)
            g.memset(mpad[:], 0.0).then_inc(pool_consts, 1)
            g.memset(v9[:], 1.0).then_inc(pool_consts, 1)
            g.memset(zeros[:], 0.0).then_inc(pool_consts, 1)
            g.memset(GT[:], 1.0).then_inc(pool_consts, 1)
            pool.wait_ge(pool_consts, 8)
            pool.wait_ge(loaded, 16 * len(loads))

            def root_x(i):
                pool.wait_ge(v_ln.sem, v_ln.at(i, 3))
                g.tensor_tensor(rstd[:], mv[:, :, 1], neg_half[:, 0:1].to_broadcast([P, NT]),
                                ALU.pow).then_inc(p_rstd.sem, 1)

            def root(i, t):
                pool.wait_ge(v_ms.sem, v_ms.at(i, 3 * t + 3))
                g.tensor_tensor(fo[:, t, :], ms[:, t, :], neg_half[:, 0:1].to_broadcast([P, H]), ALU.pow)\
                    .then_inc(p_f.sem, 1)

            def normalise(j, t):
                pool.wait_ge(p_f.sem, p_f.at(j, t + 1))
                g.tensor_tensor(O[t], O[t], bc(fo[:, t, :], DH), ALU.mult).then_inc(p_on.sem, 1)
                pool.wait_ge(p_on.sem, p_on.at(j, 2 * t + 1))
                g.tensor_tensor(O[t], O[t], onorm[:].unsqueeze(1).to_broadcast([P, H, DH]), ALU.mult)\
                    .then_inc(p_on.sem, 1)

            def gdn(i, meanwhile):
                for c in range(NC):
                    meanwhile(("conv", c))
                    b = c % 2
                    pool.wait_ge(a_silu.sem, a_silu.at(i, c + 1))
                    if begun(i, c - 1):
                        pool.wait_ge(sums_done.sem, sums_done.at(i, c - 1))
                    g.tensor_tensor(sq[:, b, 2, :], qs[:, b, 0, :], qs[:, b, 1, :], ALU.mult).then_inc(p_sq.sem, 1)
                    if begun(i, c - 1):
                        pool.wait_ge(v_QK.sem, v_QK.at(i, c - 1))
                    g.tensor_tensor(qc[:, b], qs[:, b], cos[:].unsqueeze(1).to_broadcast([P, 2, T]),
                                    ALU.mult).then_inc(p_rope.sem, 1)
                    pool.wait_ge(v_rot.sem, v_rot.at(i, c + 1))
                    g.tensor_tensor(rot[:, b], rot[:, b], sin[:].unsqueeze(1).to_broadcast([P, 2, T]),
                                    ALU.mult).then_inc(p_rope.sem, 1)
                meanwhile(("conv", NC))
                pool.wait_ge(v_sum.sem, v_sum.at(i, 2))
                g.tensor_tensor(nrm[:], sk[:, :, 1, :], half_c[:, 0:1].unsqueeze(1).to_broadcast([P, NT, H]),
                                ALU.pow).then_inc(p_nrm.sem, 1)
                pool.wait_ge(p_nrm.sem, p_nrm.at(i, 1))
                pool.wait_ge(a_V.sem, a_V.at(i, 4))
                for t in range(NT):
                    g.tensor_tensor(V[:, t], V[:, t], bc(nrm[:, t, :], DH), ALU.mult).then_inc(p_V.sem, 1)
                pool.wait_ge(v_Kt.sem, v_Kt.at(i, 3))
                carry_waits(pool)
                g.memset(X, 0.0).then_inc(p_blk.sem, 1)
                pool.wait_ge(p_blk.sem, p_blk.at(i, 1))
                carry_waits(pool)
                g.memset(X.rearrange("p t c -> p (t c)")[:, ::SB + 1], 1.0).then_inc(p_blk.sem, 1)
                pool.wait_ge(v_blk.sem, v_blk.at(i, 1))
                for r in range(SPLIT, SB - 1):
                    n, w, signalled = SB - 1 - r, r + 1 - SPLIT, 2 + 2 * (r - SPLIT)
                    pool.wait_ge(p_blk.sem, p_blk.at(i, signalled))
                    tmp_ = tmpp.rearrange("p a b -> p (a b)")[:, 0:n * w].rearrange("p (a b) -> p a b", a=n)
                    g.tensor_tensor(tmp_, Eb[:, r + 1:, r:r + 1].to_broadcast([P, n, w]),
                                    X[:, r:r + 1, SPLIT:r + 1].to_broadcast([P, n, w]), ALU.mult).then_inc(p_blk.sem, 1)
                    pool.wait_ge(p_blk.sem, p_blk.at(i, signalled + 1))
                    g.tensor_tensor(X[:, r + 1:, SPLIT:r + 1], X[:, r + 1:, SPLIT:r + 1], tmp_, ALU.subtract)\
                        .then_inc(p_blk.sem, 1)
                meanwhile(("block", SB - 2))
                meanwhile("join")
                pool.wait_ge(p_blk.sem, p_blk.at(i, p_blk.per))
                pool.wait_ge(v_sum.sem, v_sum.at(i, 6))
                pool.wait_ge(a_T1.sem, a_T1.at(i, 2))
                pool.wait_ge(p_V.sem, p_V.at(i, 2))
                g.tensor_tensor(Dv[:], V[:, 0], bc(dd[:, 0, :], DH), ALU.mult).then_inc(p_Dv.sem, 1)
                meanwhile("S")
                for half in range(2):
                    pool.wait_ge(v_R.sem, v_R.at(i, 3 + half))
                    g.tensor_tensor(R[:, PARITY[half], :], V[:, 1, PARITY[half], :], R[:, PARITY[half], :],
                                    ALU.subtract).then_inc(p_R1.sem, 1)
                pool.wait_ge(v_O.sem, v_O.at(i, 2))
                g.tensor_tensor(Dv[:], V[:, 1], bc(dd[:, 1, :], DH), ALU.mult).then_inc(p_Dv.sem, 1)
                if begun(i, 0):
                    pool.wait_ge(v_moe.sem, v_moe.at((i, 1), 1))
                carry_waits(pool)
                g.tensor_copy(x1[:], xin[:]).then_inc(p_x1.sem, 1)
                pool.wait_ge(p_Dv.sem, p_Dv.at(i, 2))
                for half in range(2):
                    pool.wait_ge(v_QS.sem, v_QS.at(i, half + 1))
                    g.tensor_tensor(Dv[:, PARITY[half], :], Dv[:, PARITY[half], :], Kt[:, PARITY[half], :],
                                    ALU.add).then_inc(p_Dv.sem, 1)
                root(i, 0)
                normalise(i, 0)
                root_x((i, -1))
                root(i, 1)
                meanwhile(None)

            def ffn(j, step, n):
                if step == "norm":
                    normalise(j, 1)
                elif step in ("ln", "fWo"):
                    for k in (0, 1) if step == "ln" else (2,):
                        pool.wait_ge(f_ln.sem, f_ln.at(j, 5 * k + 3))
                        g.tensor_tensor(frstd[:], fmv[:, :, 1], neg_half[:, 0:1].to_broadcast([P, NT]),
                                        ALU.pow).then_inc(fp_rstd.sem, 1)
                elif step == "b2":
                    g.tensor_tensor(x1[:], x1[:], x2[:], ALU.add).then_inc(p_xs.sem, 1)

            batches(pool, gdn, ffn, lambda: root_x(0))


        @block.scalar
        def _(act):
            s = nc.scalar
            act.wait_ge(loaded, 16 * len(loads))
            s.copy(identb[:], ident[:]).then_inc(act_consts, 1)
            s.copy(alpha_sel[:], stage[:, 0:H * P]).then_inc(act_consts, 1)
            s.copy(q_sel[:].rearrange("p a b c -> p (a b c)"), stage[:, H * P:H * P + n_q]).then_inc(act_consts, 1)
            s.copy(k_sel[:].rearrange("p a b c -> p (a b c)"), stage[:, H * P + n_q:H * P + 2 * n_q])\
                .then_inc(act_consts, 1)
            s.activation(neg_A[:], A_log[:], ACT.Exp).then_inc(act_consts, 1)
            act.wait_ge(act_consts, 5)
            s.mul(neg_A[:], neg_A[:], -1.0).then_inc(act_consts, 1)

            def first_tap(i, n):
                use = ("qk", n) if n < NC else ("v", n - NC)
                which = ((0, n), (1, n)) if n < NC else ((2, 2 * (n - NC)), (2, 2 * (n - NC) + 1))
                act.wait_ge(*full_at(i, use))
                ps = pair(bank(use))
                if begun(i, n - 1):
                    act.wait_ge(a_silu.sem, a_silu.at(i, n - 1))
                if n == 0 and begun(i, 0):
                    act.wait_ge(v_ms.sem, v_ms.at(i, 0))
                for m, (kind, c) in enumerate(which):
                    ins = s.activation(acc[:, n % 2, m, :], ps[:, m, :], ACT.Identity,
                                       bias=conv_b[:, kind, c:c + 1], scale=conv_w[:, kind, c, PAD:KT])
                ins.then_inc(a_acc.sem, 1)

            def silu(i, n):
                act.wait_ge(v_conv.sem, v_conv.at(i, 6 * (n + 1)))
                if n < NC:
                    if begun(i, 2 * n - 3):
                        act.wait_ge(p_rope.sem, p_rope.at(i, 2 * n - 3))
                    if begun(i, n - 1):
                        act.wait_ge(v_rot.sem, v_rot.at(i, n - 1))
                    s.activation(qs[:, n % 2], acc[:, n % 2], ACT.Silu).then_inc(a_silu.sem, 1)
                    act.wait_ge(a_silu.sem, a_silu.at(i, n + 1))
                    if begun(i, n - 1):
                        act.wait_ge(sums_done.sem, sums_done.at(i, n - 1))
                    s.activation(sq[:, n % 2, 0:2, :], qs[:, n % 2], ACT.Square).then_inc(a_sq.sem, 1)
                else:
                    m = n - NC
                    s.activation(vs[:, 2 * m:2 * m + 2, :], acc[:, n % 2], ACT.Silu).then_inc(a_silu.sem, 1)

            def square(i, t):
                act.wait_ge(v_O.sem, v_O.at(i, 2 * t + 2))
                s.activation(squares[t], O[t], ACT.Square).then_inc(a_osq.sem, 1)

            def gdn(i, meanwhile):
                act.wait_ge(*full_at(i, "xT"))
                ps = bank("xT")
                s.copy(xnT[:], ps[:, 0:T]).then_inc(xnT_ready.sem, 1)
                act.wait_ge(v_gate.sem, v_gate.at(i, 3))
                s.activation(eabs[:], nabs[:], ACT.Exp).then_inc(a_gate.sem, 1)
                s.activation(emin[:], zmin[:], ACT.Exp).then_inc(a_gate.sem, 1)
                for n in range(NCONV + 1):
                    if n < NCONV:
                        first_tap(i, n)
                    if n == 1:
                        act.wait_ge(v_gate.sem, v_gate.at(i, 20))
                        s.activation(alpha[:], lpp[:], ACT.Exp).then_inc(a_gate.sem, 1)
                    if n >= 1:
                        silu(i, n - 1)
                    if n == NC + SUMS_LAG:
                        act.wait_ge(sums_done.sem, sums_done.at(i, NC))
                        s.copy(sumsT[0:3 * SB], bank("sums")[0:3 * SB, 0:T]).then_inc(a_sums.sem, 1)
                    meanwhile(("conv", n))
                for half in range(2):
                    for t in range(NT):
                        act.wait_ge(*full_at(i, ("vT", t, half)))
                        if begun(i, 0):
                            act.wait_ge(v_y.sem, v_y.at(i, 0))
                        s.copy(V[:, t, HALF[half], :], by_head(bank(("vT", t, half)))).then_inc(a_V.sem, 1)
                for n, heads in enumerate(QUARTERS):
                    meanwhile(("head", heads - 2))
                    act.wait_ge(v_Kt.sem, v_Kt.at(i, n + 1))
                    for q in range(P // SB):
                        units = NP[ROWS[q], :, 1, ROWS[q]].rearrange("p (t h) k -> p k t h", t=NT)
                        ins = s.copy(Dg[ROWS[q]].rearrange("p k (t h) -> p k t h", t=NT)[:, :, :, heads - 4:heads],
                                     units[:, :, :, heads - 4:heads])
                    ins.then_inc(a_diag.sem, 1)
                meanwhile("kT")
                meanwhile(("block", SB - 2))
                for half in range(2):
                    act.wait_ge(*full_at(i, ("join1", half)))
                    ps = bank(("join1", half))
                    for q in (1, 3):
                        ins = s.copy(T1[ROWS[q], 16 * half:16 * half + 16, :], by_unit(ps)[ROWS[q]])
                    ins.then_inc(a_T1.sem, 1)
                for half in range(2):
                    act.wait_ge(*full_at(i, ("join2", half)))
                    ps = bank(("join2", half))
                    for q in (0, 2):
                        ins = s.mul(Z[ROWS[q], 16 * half:16 * half + 16, SB:2 * SB], by_unit(ps)[ROWS[q]], -1.0)
                    ins.then_inc(a_Z.sem, 1)
                meanwhile("join")
                for t in range(NT):
                    for what, rows in (("top", slice(0, DH)), ("low", slice(DH, P))):
                        for half in range(2):
                            act.wait_ge(*full_at(i, (what, t, half)))
                            ps = bank((what, t, half))
                            s.copy(W[t][rows, HALF[half], :], by_head(ps)[rows]).then_inc(a_W.sem, 1)
                        if t and what == "low":
                            square(i, 0)
                        meanwhile((what, t))
                        if what == "top":
                            meanwhile(("cross", t))
                    if t == 0:
                        act.wait_ge(*full_at(i, "S"))
                        ps = bank("S")
                        s.copy(S[:], by_head(ps)).then_inc(a_S.sem, 1)
                        meanwhile("S")
                        meanwhile(("o", 0))
                meanwhile(("o", 1))
                square(i, 1)
                for t in range(NT):
                    for half in range(2):
                        act.wait_ge(*full_at(i, ("g", t, half)))
                        s.copy(V[:, t, HALF[half], :], by_head(bank(("g", t, half)))).then_inc(a_g.sem, 1)
                meanwhile(None)

            def context(j, half):
                act.wait_ge(pv_done.sem, pv_done.at(j, 2 * half + 2))
                s.copy(ctx9[:, 2 * half:2 * half + 2, :], pair(bank(("pv", half)))).then_inc(a_ctx9.sem, 1)

            def ffn(j, step, n):
                if step == "silu":
                    for t in range(NT):
                        act.wait_ge(p_on.sem, p_on.at(j, 2 * t + 2))
                        s.activation(O[t], O[t], ACT.Silu).then_inc(a_sg.sem, 1)
                elif step == "yT":
                    for half in range(2):
                        act.wait_ge(*full_at(j, ("yT", n, half)))
                        s.copy(yT[n][:, 4 * half:4 * half + 4, :],
                               bank(("yT", n, half))[:].rearrange("p (c k) -> p c k", c=4)).then_inc(a_yT.sem, 1)
                elif step == "hT":
                    act.wait_ge(*full_at(j, "hT"))
                    s.activation(hT[:], bank("hT")[:, 0:T], ACT.Identity, bias=ln_gb[:, 1:2], scale=ln_gb[:, 0:1])\
                        .then_inc(a_hT.sem, 1)
                elif step == "rep":
                    act.wait_ge(*full_at(j, ("rep", n)))
                    ps = pair(bank(("rep", n)))
                    s.copy(QK6[:, n, 0, :], ps[:, 0, :]).then_inc(a_QK6.sem, 1)
                    s.activation(QK6[:, n, 1, :], ps[:, 1, :], ACT.Identity, bias=k_ones[:, 0:1])\
                        .then_inc(a_QK6.sem, 1)
                elif step == "att" and n < FH:
                    act.wait_ge(*full_at(j, ("st", n)))
                    if begun(j, n - 3):
                        act.wait_ge(pv_done.sem, pv_done.at(j, n // 4))
                    s.activation(pT[:, n % 4], pair(bank(("st", n))), ACT.Exp, scale=float(FD) ** -0.5)\
                        .then_inc(a_pT.sem, 1)
                    if n == 11:
                        context(j, 0)
                elif step == "ctx" and n == 0:
                    context(j, 1)
                elif step == "ctxT":
                    act.wait_ge(*full_at(j, "ctxT"))
                    s.copy(ctxT[:], bank("ctxT")[:, 0:T]).then_inc(a_ctxT.sem, 1)
                elif step == "mT":
                    act.wait_ge(*full_at(j, "mT"))
                    s.activation(mT[:], bank("mT")[:, 0:T], ACT.Identity, bias=ln_gb[:, 3:4], scale=ln_gb[:, 2:3])\
                        .then_inc(a_hT.sem, 1)
                elif step == "router":
                    act.wait_ge(v_lg.sem, v_lg.at(j, 2))
                    s.activation(ex[:], lg[:], ACT.Exp).then_inc(a_ex.sem, 1)
                elif step == "up":
                    for m in range(2):
                        act.wait_ge(*full_at(j, ("h1", n, m)))
                        ps = pair(bank(("h1", n, m)))
                        if n >= 2:
                            act.wait_ge(*full_at(j, ("y", n - 2)))
                        for q in range(2):
                            f = 2 * m + q
                            ins = s.activation(h1[:, n % 2, f, :], ps[:, q, :], ACT.Gelu_apprx_tanh,
                                               bias=b1[:, n, f:f + 1])
                        ins.then_inc(a_h1.sem, 1)

            batches(act, gdn, ffn)


        @block.tensor
        def _(pe):
            mm = nc.tensor.matmul

            def product(out_, lhsT, rhs, first=True, last=True):
                return mm(out_, lhsT, rhs, start=first, stop=last)

            def turn(out_, in_, n=P):
                return nc.tensor.transpose(out_, in_, ident[0:n, 0:n])

            pe.wait_ge(loaded, 16 * len(loads))
            pe.wait_ge(pool_consts, 8)
            pe.wait_ge(act_consts, 6)

            def sums(i, c):
                if c == 0 and reused(i, "sums"):
                    pe.wait_ge(*free_at(i, "sums"))
                ps = bank("sums")
                pe.wait_ge(a_sq.sem, a_sq.at(i, c + 1))
                pe.wait_ge(p_sq.sem, p_sq.at(i, c + 1))
                for kind in range(3):
                    ins = product(ps[ROWS[kind], 0:T], head_cols[:, H - 2 - 2 * c:H - 2 - 2 * c + SB],
                                  sq[:, c % 2, kind, :], c == 0, c == NC - 1)
                ins.then_inc(sums_done.sem, 1)

            def with_state(i, what, kind, half):
                pe.wait_ge(a_S.sem, a_S.at(i, 1))
                if reused(i, (what, half)):
                    pe.wait_ge(*free_at(i, (what, half)))
                ps = bank((what, half))
                for k in range(8):
                    h = 2 * k + half
                    ins = product(by_head(ps)[:, k, :], QK[rows_of(h), h // 2, kind, TOK[1]],
                                  S[rows_of(h), h // 2, :])
                ins.then_inc(full((what, half)), 1)

            def gdn(i, meanwhile):
                pe.wait_ge(v_ln.sem, v_ln.at(i, 5))
                if reused(i, "xT"):
                    pe.wait_ge(*free_at(i, "xT"))
                ps = bank("xT")
                for t in range(NT):
                    ins = turn(ps[:, TOK[t]], xn[:, t, :])
                ins.then_inc(full("xT"), 1)
                pe.wait_ge(xnT_ready.sem, xnT_ready.at(i, 1))
                if reused(i, "gate"):
                    pe.wait_ge(*free_at(i, "gate"))
                ps = bank("gate")
                for t in range(NT):
                    ins = product(ps[:, t * 2 * H:(t + 1) * 2 * H], xnT[:, TOK[t]], Wgate[:])
                ins.then_inc(full("gate"), 1)
                for n in range(NCONV + 2):
                    if n == 4:
                        pe.wait_ge(a_gate.sem, a_gate.at(i, 3))
                        if reused(i, "alphaT"):
                            pe.wait_ge(*free_at(i, "alphaT"))
                        ps = bank("alphaT")
                        for t in range(NT):
                            ins = turn(ps[0:H, TOK[t]], alpha[:, t, :])
                        ins.then_inc(full("alphaT"), 1)
                    if n == 6:
                        pe.wait_ge(v_alpha.sem, v_alpha.at(i, 7))
                        if reused(i, "GT"):
                            pe.wait_ge(*free_at(i, "GT"))
                        ps = bank("GT")
                        carry_waits(pe)
                        turn(ps[:, 0:H], GT[:, 1:GW], H)
                        turn(ps[:, H:2 * H], GT[:, 0:P], H).then_inc(full("GT"), 1)
                    if n < NCONV:
                        use = ("qk", n) if n < NC else ("v", n - NC)
                        which = ((0, n), (1, n)) if n < NC else ((2, 2 * (n - NC)), (2, 2 * (n - NC) + 1))
                        if reused(i, use):
                            pe.wait_ge(*free_at(i, use))
                        ps = pair(bank(use))
                        for m, (kind, c) in enumerate(which):
                            ins = product(ps[:, m, :], Wqkv[:, kind, c * P:(c + 1) * P], xnT[:])
                        ins.then_inc(full(use), 1)
                    if SUMS_LAG <= n < NC + SUMS_LAG:
                        sums(i, n - SUMS_LAG)
                    if n == NC + SUMS_LAG + 1:
                        pe.wait_ge(a_sums.sem, a_sums.at(i, 1))
                        for t in range(NT):
                            ins = turn(bank("sums")[:, T + t * 3 * SB:T + (t + 1) * 3 * SB], sumsT[0:3 * SB, TOK[t]], 3 * SB)
                        ins.then_inc(full("sums"), 1)
                    meanwhile(("conv", n))
                for half in range(2):
                    pe.wait_ge(a_silu.sem, a_silu.at(i, NC + 2 * half + 2))
                    for t in range(NT):
                        if reused(i, ("vT", t, half)):
                            pe.wait_ge(*free_at(i, ("vT", t, half)))
                        ps = bank(("vT", t, half))
                        for c in range(4):
                            ins = turn(ps[:, c * P:(c + 1) * P], vs[:, 4 * half + c, TOK[t]])
                        ins.then_inc(full(("vT", t, half)), 1)
                for h in range(H):
                    c, rows = h // 2, rows_of(h)
                    if reused(i, ("alpha", h)):
                        pe.wait_ge(*free_at(i, ("alpha", h)))
                    ps = bank(("alpha", h))
                    pe.wait_ge(v_alpha.sem, v_alpha.at(i, 7))
                    product(ps[:, 0:NT * GW], alpha_sel[:, h * P:(h + 1) * P],
                            alpha3[:].rearrange("p t w -> p (t w)")).then_inc(full(("alpha", h)), 1)
                    if reused(i, ("kk", h)):
                        pe.wait_ge(*free_at(i, ("kk", h)))
                    ps = bank(("kk", h))
                    pe.wait_ge(v_QK.sem, v_QK.at(i, c + 1))
                    for t in range(NT):
                        ins = product(ps[:, t * T:(t + 1) * T].rearrange("p (a k) -> p a k", a=2),
                                      QK[rows, c, 1, TOK[t]], QK[rows, c, :, TOK[t]])
                    ins.then_inc(full(("kk", h)), 1)
                    meanwhile(("head", h))
                for half in range(2):
                    if reused(i, ("kT", half)):
                        pe.wait_ge(*free_at(i, ("kT", half)))
                    ps = bank(("kT", half))
                    for c in range(4):
                        ins = turn(ps[:, c * P:(c + 1) * P], QK[:, 4 * half + c, 1, 0:P])
                    ins.then_inc(full(("kT", half)), 1)
                meanwhile("kT")
                meanwhile(("block", SB - 2))
                pe.wait_ge(v_blk.sem, v_blk.at(i, v_blk.per - 4))
                for half in range(2):
                    if reused(i, ("join1", half)):
                        pe.wait_ge(*free_at(i, ("join1", half)))
                    ps = bank(("join1", half))
                    carry_waits(pe)
                    for u in range(16):
                        for q in (0, 2):
                            ins = product(by_unit(ps)[ROWS[q + 1], u, :], NP[ROWS[q], 16 * half + u, 1, ROWS[q + 1]],
                                          XB[ROWS[q], :, 16 * half + u])
                    ins.then_inc(full(("join1", half)), 1)
                for half in range(2):
                    if reused(i, ("join2", half)):
                        pe.wait_ge(*free_at(i, ("join2", half)))
                    ps = bank(("join2", half))
                    pe.wait_ge(v_blk.sem, v_blk.at(i, v_blk.per))
                    pe.wait_ge(a_T1.sem, a_T1.at(i, half + 1))
                    carry_waits(pe)
                    for u in range(16):
                        for q in (0, 2):
                            ins = product(by_unit(ps)[ROWS[q], u, :], T1[ROWS[q + 1], 16 * half + u, :],
                                          Z[ROWS[q + 1], 16 * half + u, SB:2 * SB])
                    ins.then_inc(full(("join2", half)), 1)
                meanwhile("join")
                pe.wait_ge(p_V.sem, p_V.at(i, 2))
                top, low = slice(0, DH), slice(DH, P)
                for t in range(NT):
                    right = V[:, 0] if t == 0 else R[:]
                    for half in range(2):
                        if reused(i, ("top", t, half)):
                            pe.wait_ge(*free_at(i, ("top", t, half)))
                        ps = bank(("top", t, half))
                        if t:
                            pe.wait_ge(p_R1.sem, p_R1.at(i, 2))
                        carry_waits(pe)
                        for k in range(8):
                            h = 8 * half + k
                            ins = product(by_head(ps)[top, k, :], Z[top, t * H + h, :], right[top, h, :])
                        ins.then_inc(full(("top", t, half)), 1)
                    if t:
                        with_state(i, "QS", 0, 0)
                    meanwhile(("top", t))
                    for half in range(2):
                        if reused(i, ("cross", t, half)):
                            pe.wait_ge(*free_at(i, ("cross", t, half)))
                        ps = bank(("cross", t, half))
                        pe.wait_ge(a_W.sem, a_W.at(i, 4 * t + half + 1))
                        carry_waits(pe)
                        for k in range(8):
                            h = 8 * half + k
                            ins = product(by_head(ps)[low, k, :], NP[top, t * H + h, 1, DH:P], W[t][top, h, :])
                        ins.then_inc(full(("cross", t, half)), 1)
                    if t:
                        with_state(i, "QS", 0, 1)
                    meanwhile(("cross", t))
                    for half in range(2):
                        if reused(i, ("low", t, half)):
                            pe.wait_ge(*free_at(i, ("low", t, half)))
                        ps = bank(("low", t, half))
                        pe.wait_ge(v_R.sem, v_R.at(i, 4 * t + half + 1))
                        carry_waits(pe)
                        for k in range(8):
                            h = 8 * half + k
                            ins = product(by_head(ps)[low, k, :], Z[low, t * H + h, :], R[low, h, :])
                        ins.then_inc(full(("low", t, half)), 1)
                    meanwhile(("low", t))
                    if t == 0:
                        if reused(i, "S"):
                            pe.wait_ge(*free_at(i, "S"))
                        ps = bank("S")
                        pe.wait_ge(v_Kt.sem, v_Kt.at(i, 6))
                        pe.wait_ge(a_W.sem, a_W.at(i, 4))
                        for h in range(H):
                            ins = product(by_head(ps)[rows_of(h), h // 2, :], Kt[:, h, :], W[0][:, h, :])
                        ins.then_inc(full("S"), 1)
                        for half in range(2):
                            with_state(i, "KS", 1, half)
                        meanwhile("S")
                    for half in range(2):
                        if reused(i, ("o", t, half)):
                            pe.wait_ge(*free_at(i, ("o", t, half)))
                        ps = bank(("o", t, half))
                        pe.wait_ge(a_W.sem, a_W.at(i, 4 * t + half + 3))
                        for k in range(8):
                            h = 8 * half + k
                            ins = product(by_head(ps)[:, k, :], NP[:, t * H + h, 0, :], W[t][:, h, :])
                        ins.then_inc(full(("o", t, half)), 1)
                    meanwhile(("o", t))
                for t in range(NT):
                    for half in range(2):
                        if reused(i, ("g", t, half)):
                            pe.wait_ge(*free_at(i, ("g", t, half)))
                        ps = bank(("g", t, half))
                        product(ps[:], xnT[:, TOK[t]], Wg[:, half * 512:(half + 1) * 512])\
                            .then_inc(full(("g", t, half)), 1)
                meanwhile(None)

            def ffn(j, step, n):
                use = (step, n) if step in ("rep", "max", "mrow", "ctx") else step
                if step in ("Wo", "hT", "fqk", "fv", "rep", "max", "mrow", "ctx", "ctxT", "fWo", "mT", "router",
                            "wT", "b2"):
                    if reused(j, use):
                        pe.wait_ge(*free_at(j, use))
                    ps = bank(use)
                if step == "yT":
                    for half in range(2):
                        if reused(j, ("yT", n, half)):
                            pe.wait_ge(*free_at(j, ("yT", n, half)))
                        pe.wait_ge(v_y.sem, v_y.at(j, n + 1))
                        for c in range(4):
                            h = 8 * half + 2 * c
                            ins = turn(bank(("yT", n, half))[:, c * P:(c + 1) * P],
                                       O[n][:, h:h + 2, :].rearrange("p h d -> p (h d)"))
                        ins.then_inc(full(("yT", n, half)), 1)
                elif step == "Wo":
                    for t in range(NT):
                        pe.wait_ge(a_yT.sem, a_yT.at(j, 2 * t + 2))
                        for c in range(NC):
                            ins = product(ps[:, TOK[t]], yT[t][:, c, :], Wo[:, c, :], c == 0, c == NC - 1)
                    ins.then_inc(full("Wo"), 1)
                elif step == "hT":
                    pe.wait_ge(f_ln.sem, f_ln.at(j, 10))
                    for t in range(NT):
                        ins = turn(ps[:, TOK[t]], hn[:, t, :])
                    ins.then_inc(full("hT"), 1)
                elif step == "fqk":
                    pe.wait_ge(a_hT.sem, a_hT.at(j, 1))
                    product(pair(ps)[:, 0, :], fW[:, 0, :], hT[:])
                    product(pair(ps)[:, 1, :], fW[:, 1, :], hT[:]).then_inc(full("fqk"), 1)
                elif step == "fv":
                    for t in range(NT):
                        ins = product(ps[:, TOK[t]], hT[:, TOK[t]], fW[:, 2, :])
                    ins.then_inc(full("fv"), 1)
                elif step == "rep":
                    pe.wait_ge(v_part.sem, v_part.at(j, 4))
                    for kind, sel in ((0, q_sel), (1, k_sel)):
                        for s in range(NS):
                            ins = product(pair(ps)[:, kind, :], sel[:, s, n, :], part[:, s, kind, :],
                                          s == 0, s == NS - 1)
                    ins.then_inc(full(("rep", n)), 1)
                elif step == "max":
                    c, rows = n // 2, rows_of(n)
                    pe.wait_ge(a_QK6.sem, a_QK6.at(j, 2 * c + 2))
                    for t in range(NT):
                        ins = product(pair(ps)[:, t, :], QK6[rows, c, 0, TOK[t]], QK6[rows, c, 1, :])
                    ins.then_inc(full(("max", n)), 1)
                elif step == "mrow":
                    pe.wait_ge(v_mp.sem, v_mp.at(j, 5))
                    for q in range(2):
                        c = 2 * n + q
                        for t in range(NT):
                            ins = product(pair(ps)[:, q, TOK[t]],
                                          mpad[:, t, 2 * c:2 * c + 2, :].rearrange("p h d -> p (h d)"), identb[:])
                    ins.then_inc(full(("mrow", n)), 1)
                elif step == "att":
                    if n < FH:
                        c, rows = n // 2, rows_of(n)
                        if reused(j, ("st", n)):
                            pe.wait_ge(*free_at(j, ("st", n)))
                        for kt in range(NT):
                            ins = product(pair(bank(("st", n)))[:, kt, :], QK6[rows, c, 1, TOK[kt]],
                                          QK6[rows, c, 0, :])
                        ins.then_inc(full(("st", n)), 1)
                    if n % 4 == 0 and n:
                        group = n // 4 - 1
                        half, slot = group // 2, group % 2
                        if slot == 0 and reused(j, ("pv", half)):
                            pe.wait_ge(*free_at(j, ("pv", half)))
                        pe.wait_ge(v_v9.sem, v_v9.at(j, 1))
                        pe.wait_ge(a_pT.sem, a_pT.at(j, n))
                        for kt in range(NT):
                            for q in range(4):
                                at = (kt * FH + 4 * group + q) * (FD + 1)
                                ins = product(pair(bank(("pv", half)))[ROWS[q], slot, :], v9[:, at:at + SB],
                                              pT[:, q, kt, :], kt == 0, kt == NT - 1)
                        ins.then_inc(pv_done.sem, 1)
                elif step == "ctx":
                    pe.wait_ge(a_ctx9.sem, a_ctx9.at(j, 2))
                    for group in range(4):
                        ins = turn(ps[:, group * P:(group + 1) * P], ctx9[:, group, TOK[n]])
                    ins.then_inc(full(("ctx", n)), 1)
                elif step == "ctxT":
                    pe.wait_ge(v_ctx.sem, v_ctx.at(j, 2 * NT))
                    for t in range(NT):
                        ins = turn(ps[:, TOK[t]], ctxn[:, t, :])
                    ins.then_inc(full("ctxT"), 1)
                elif step == "fWo":
                    pe.wait_ge(a_ctxT.sem, a_ctxT.at(j, 1))
                    for t in range(NT):
                        ins = product(ps[:, TOK[t]], ctxT[:, TOK[t]], fW[:, 3, :])
                    ins.then_inc(full("fWo"), 1)
                elif step == "mT":
                    pe.wait_ge(f_ln.sem, f_ln.at(j, 15))
                    for t in range(NT):
                        ins = turn(ps[:, TOK[t]], hn[:, t, :])
                    ins.then_inc(full("mT"), 1)
                elif step == "router":
                    pe.wait_ge(a_hT.sem, a_hT.at(j, 2))
                    for t in range(NT):
                        ins = product(ps[:, t * NE:(t + 1) * NE], mT[:, TOK[t]], Wr[:])
                    ins.then_inc(full("router"), 1)
                elif step == "wT":
                    pe.wait_ge(v_w.sem, v_w.at(j, 9))
                    for t in range(NT):
                        ins = turn(ps[0:NE, TOK[t]], wsel[:, t, :])
                    ins.then_inc(full("wT"), 1)
                elif step == "b2":
                    pe.wait_ge(v_wT.sem, v_wT.at(j, 1))
                    for t in range(NT):
                        ins = product(ps[:, TOK[t]], wT[:, TOK[t]], b2[:])
                    ins.then_inc(full("b2"), 1)
                elif step == "up":
                    for m in range(2):
                        if reused(j, ("h1", n, m)):
                            pe.wait_ge(*free_at(j, ("h1", n, m)))
                        ps = pair(bank(("h1", n, m)))
                        for q in range(2):
                            f = 2 * m + q
                            ins = product(ps[:, q, :], W1[:, n, f * P:(f + 1) * P], mT[:])
                        ins.then_inc(full(("h1", n, m)), 1)
                elif step == "down":
                    if reused(j, ("y", n)):
                        pe.wait_ge(*free_at(j, ("y", n)))
                    pe.wait_ge(a_h1.sem, a_h1.at(j, 2 * n + 2))
                    ps = bank(("y", n))
                    for t in range(NT):
                        for f in range(NF):
                            ins = product(ps[:, TOK[t]], h1[:, n % 2, f, TOK[t]], W2[:, n, f, :],
                                          f == 0, f == NF - 1)
                    ins.then_inc(full(("y", n)), 1)

            batches(pe, gdn, ffn)


        @block.vector
        def _(dve):
            v = nc.vector
            dve.wait_ge(loaded, 16 * len(loads))
            v.tensor_tensor(gate_bias[:, H:2 * H], gate_bias[:, H:2 * H], dt_bias[:], ALU.add).then_inc(vec_consts, 1)
            dve.wait_ge(vec_consts, 1)
            dve.wait_ge(pool_consts, 8)
            dve.wait_ge(act_consts, 6)

            def layer_norm(i, x_, st, mv_, rs, out_, sig, k, rsig, rk):
                for t in range(NT):
                    ins = v.bn_stats(st[:, t, :], x_[:, t, :])
                ins.then_inc(sig.sem, 1)
                dve.wait_ge(sig.sem, sig.at(i, k + 1))
                carry_waits(dve)
                for t in range(NT):
                    ins = v.bn_aggr(mv_[:, t, :], st[:, t, :])
                ins.then_inc(sig.sem, 1)
                dve.wait_ge(sig.sem, sig.at(i, k + 2))
                v.tensor_scalar(mv_[:, :, 1], mv_[:, :, 1], EPS_LN, None, ALU.add).then_inc(sig.sem, 1)
                dve.wait_ge(rsig.sem, rsig.at(i, rk))
                for t in range(NT):
                    v.tensor_scalar(out_[:, t, :], x_[:, t, :], mv_[:, t, 0:1], rs[:, t:t + 1], ALU.subtract,
                                    ALU.mult).then_inc(sig.sem, 1)

            def conv(i, n):
                use = ("qk", n) if n < NC else ("v", n - NC)
                which = ((0, n), (1, n)) if n < NC else ((2, 2 * (n - NC)), (2, 2 * (n - NC) + 1))
                dve.wait_ge(*full_at(i, use))
                ps = pair(bank(use))
                dve.wait_ge(a_acc.sem, a_acc.at(i, n + 1))
                for j in range(1, KT):
                    for m, (kind, c) in enumerate(which):
                        if j > 1:
                            dve.wait_ge(v_conv.sem, v_conv.at(i, 6 * n + 2 * (j - 2) + m + 1))
                        v.scalar_tensor_tensor(acc[:, n % 2, m, j:T], ps[:, m, 0:T - j],
                                               conv_w[:, kind, c, PAD - j:KT - j], acc[:, n % 2, m, j:T],
                                               ALU.mult, ALU.add).then_inc(v_conv.sem, 1)

            def gate(i):
                dve.wait_ge(a_gate.sem, a_gate.at(i, 2))
                v.tensor_scalar(den[:, :, 0:H], eabs[:, :, 0:H], 1.0, None, ALU.add).then_inc(v_gate.sem, 1)
                v.tensor_scalar(den[:, :, H:2 * H], eabs[:, :, H:2 * H], 2.0, None, ALU.add).then_inc(v_gate.sem, 1)
                dve.wait_ge(v_gate.sem, v_gate.at(i, 5))
                v.reciprocal(den[:], den[:]).then_inc(v_gate.sem, 1)
                dve.wait_ge(v_gate.sem, v_gate.at(i, 6))
                v.tensor_tensor(beta[:], emin[:], den[:, :, 0:H], ALU.mult).then_inc(v_gate.sem, 1)
                v.tensor_tensor(lp[:], eabs[:, :, H:2 * H], den[:, :, H:2 * H], ALU.mult).then_inc(v_gate.sem, 1)
                dve.wait_ge(v_gate.sem, v_gate.at(i, 8))
                v.tensor_tensor(lp2[:], lp[:], lp[:], ALU.mult).then_inc(v_gate.sem, 1)
                dve.wait_ge(v_gate.sem, v_gate.at(i, 9))
                v.tensor_scalar(lpp[:], lp2[:], 1.0 / 15, None, ALU.mult).then_inc(v_gate.sem, 1)
                for n, d in enumerate((13, 11, 9, 7, 5, 3)):
                    dve.wait_ge(v_gate.sem, v_gate.at(i, 10 + n))
                    v.scalar_tensor_tensor(lpp[:], lpp[:], 1.0 / d, lp2[:], ALU.add, ALU.mult)\
                        .then_inc(v_gate.sem, 1)
                dve.wait_ge(v_gate.sem, v_gate.at(i, 16))
                v.scalar_tensor_tensor(lpp[:], lpp[:], 1.0, lp[:], ALU.add, ALU.mult).then_inc(v_gate.sem, 1)
                v.tensor_scalar(lp2[:], z[:, :, H:2 * H], 0.0, 0.5, ALU.max, ALU.mult).then_inc(v_gate.sem, 1)
                dve.wait_ge(v_gate.sem, v_gate.at(i, 18))
                v.tensor_tensor(lpp[:], lpp[:], lp2[:], ALU.add).then_inc(v_gate.sem, 1)
                dve.wait_ge(v_gate.sem, v_gate.at(i, 19))
                v.scalar_tensor_tensor(lpp[:], lpp[:], 2.0, neg_A[:].unsqueeze(1).to_broadcast([P, NT, H]),
                                       ALU.mult, ALU.mult).then_inc(v_gate.sem, 1)

            def alpha_parts(i):
                dve.wait_ge(*full_at(i, "alphaT"))
                ps = bank("alphaT")
                a_t = ps[0:H, 0:T].rearrange("p (t k) -> p t k", t=NT)
                v.tensor_copy(al1[:], a_t).then_inc(v_alpha.sem, 1)
                dve.wait_ge(v_alpha.sem, v_alpha.at(i, 1))
                v.tensor_tensor(alr[:], a_t, al1[:], ALU.subtract).then_inc(v_alpha.sem, 1)
                dve.wait_ge(v_alpha.sem, v_alpha.at(i, 2))
                v.tensor_copy(al2[:], alr[:]).then_inc(v_alpha.sem, 1)
                v.tensor_copy(alpha3[0:H, :, 2:GW], al1[:, :, 1:P]).then_inc(v_alpha.sem, 1)
                dve.wait_ge(v_alpha.sem, v_alpha.at(i, 3))
                v.tensor_copy(alpha3[32:32 + H, :, 2:GW], al2[:, :, 1:P]).then_inc(v_alpha.sem, 1)
                v.tensor_tensor(alpha3[64:64 + H, :, 2:GW], alr[:, :, 1:P], al2[:, :, 1:P], ALU.subtract)\
                    .then_inc(v_alpha.sem, 1)
                v.tensor_tensor_scan(GT[:, 1:GW], ps[0:H, P:T], zeros[:], 1.0, ALU.mult, ALU.add)\
                    .then_inc(v_alpha.sem, 1)

            def norms(i):
                dve.wait_ge(*full_at(i, "sums"))
                sums_ = bank("sums")[:, T:T + NT * 3 * SB].rearrange("p (t a h) -> p t a h", t=NT, a=3)[:, :, :, 0:H]
                v.tensor_scalar(sk[:, :, 0:2, :], sums_[:, :, 0:2, :], EPS_NORM, None, ALU.add).then_inc(v_sum.sem, 1)
                v.tensor_copy(sk[:, :, 2, :], sums_[:, :, 2, :]).then_inc(v_sum.sem, 1)
                dve.wait_ge(v_sum.sem, v_sum.at(i, 2))
                v.reciprocal(rk2[:], sk[:, :, 1, :]).then_inc(v_sum.sem, 1)
                dve.wait_ge(v_sum.sem, v_sum.at(i, 3))
                v.tensor_tensor(es[:], beta[:], rk2[:], ALU.mult).then_inc(v_sum.sem, 1)
                v.tensor_tensor(dd[:], sk[:, :, 2, :], rk2[:], ALU.mult).then_inc(v_sum.sem, 1)
                dve.wait_ge(v_sum.sem, v_sum.at(i, 5))
                v.tensor_tensor(dd[:], dd[:], D_bc[:].unsqueeze(1).to_broadcast([P, NT, H]), ALU.mult)\
                    .then_inc(v_sum.sem, 1)

            def with_state(i, half):
                dve.wait_ge(*full_at(i, ("QS", half)))
                v.tensor_tensor(Kt[:, PARITY[half], :], by_head(bank(("QS", half))), bc(Gc[:, 1, PARITY[half]], DH),
                                ALU.mult).then_inc(v_QS.sem, 1)

            def normalise_x(i):
                dve.wait_ge(x_in.sem, x_in.at(i, 16))
                layer_norm(i, xin, stats, mv, rstd, xn, v_ln, 0, p_rstd, 1)

            def mean_square(i, t):
                dve.wait_ge(a_osq.sem, a_osq.at(i, t + 1))
                v.tensor_reduce(ms[:, t, :], squares[t], AX.X, ALU.add).then_inc(v_ms.sem, 1)
                dve.wait_ge(v_ms.sem, v_ms.at(i, 3 * t + 1))
                v.scalar_tensor_tensor(ms[:, t, :], sk[:, t, 0, :], DH * EPS_NORM, ms[:, t, :], ALU.mult, ALU.add)\
                    .then_inc(v_ms.sem, 1)
                dve.wait_ge(v_ms.sem, v_ms.at(i, 3 * t + 2))
                v.tensor_scalar(ms[:, t, :], ms[:, t, :], 1.0 / DH, None, ALU.mult).then_inc(v_ms.sem, 1)

            def gdn(i, meanwhile):
                dve.wait_ge(*full_at(i, "gate"))
                ps = bank("gate")
                v.tensor_tensor(z[:], ps[:, 0:NT * 2 * H].rearrange("p (t h) -> p t h", t=NT),
                                gate_bias[:].unsqueeze(1).to_broadcast([P, NT, 2 * H]), ALU.add)\
                    .then_inc(v_gate.sem, 1)
                dve.wait_ge(v_gate.sem, v_gate.at(i, 1))
                v.scalar_tensor_tensor(nabs[:], z[:], -1.0, z[:], ALU.mult, ALU.min).then_inc(v_gate.sem, 1)
                v.tensor_scalar(zmin[:], z[:, :, 0:H], 0.0, None, ALU.min).then_inc(v_gate.sem, 1)
                swap = [p ^ 1 for p in range(32)]
                for n in range(NCONV + 1):
                    if n < NCONV:
                        conv(i, n)
                    if n == 0:
                        gate(i)
                    if n == 3:
                        alpha_parts(i)
                    if n == NC + SUMS_LAG + 1:
                        norms(i)
                    if n == 5:
                        dve.wait_ge(*full_at(i, "GT"))
                        ps = bank("GT")
                        v.tensor_copy(Gc[:].rearrange("p a h -> p (a h)"), ps[:, 0:2 * H]).then_inc(v_Gc.sem, 1)
                    if 1 <= n <= NC:
                        c = n - 1
                        dve.wait_ge(a_silu.sem, a_silu.at(i, c + 1))
                        if begun(i, c - 1):
                            dve.wait_ge(v_QK.sem, v_QK.at(i, c - 1))
                        carry_waits(dve)
                        v.stream_shuffle(rot[:, c % 2], qs[:, c % 2], swap).then_inc(v_rot.sem, 1)
                    if 2 <= n <= NC + 1:
                        c = n - 2
                        dve.wait_ge(p_rope.sem, p_rope.at(i, 2 * c + 2))
                        v.tensor_tensor(QK[:, c], qc[:, c % 2], rot[:, c % 2], ALU.add).then_inc(v_QK.sem, 1)
                    meanwhile(("conv", n))
                for h in range(H + 1):
                    if h < H:
                        dve.wait_ge(*full_at(i, ("alpha", h)))
                        ps = bank(("alpha", h))
                        v.tensor_tensor_scan(Gam[:, h, :], ps[:, 0:NT * GW], ident_pad[:], 0.0, ALU.mult, ALU.add)\
                            .then_inc(v_Gam.sem, 1)
                    if h >= 1:
                        dve.wait_ge(*full_at(i, ("kk", h - 1)))
                        ps = bank(("kk", h - 1))
                        dve.wait_ge(v_Gam.sem, v_Gam.at(i, h))
                        for t in range(NT):
                            both = bass.AP(Gam[:].tensor, (h - 1) * NT * GW + t * GW, [[H * NT * GW, P], [1, 2], [1, P]])
                            ins = v.scalar_tensor_tensor(
                                NP[:, t * H + h - 1, :, :], ps[:, t * T:(t + 1) * T].rearrange("p (a k) -> p a k", a=2),
                                es[:, t, h - 1:h], both, ALU.mult, ALU.mult)
                        ins.then_inc(v_NP.sem, 1)
                    if h in QUARTERS:
                        four = slice(h - 4, h)
                        v.tensor_tensor(fac[:, four], es[:, 0, four], Gam[:, four, P], ALU.mult).then_inc(v_Kt.sem, 1)
                    meanwhile(("head", h))
                dve.wait_ge(v_Kt.sem, v_Kt.at(i, 4))
                for half in range(2):
                    dve.wait_ge(*full_at(i, ("kT", half)))
                    ps = bank(("kT", half))
                    v.tensor_tensor(Kt[:, HALF[half], :], by_head(ps), bc(fac[:, HALF[half]], DH), ALU.mult)\
                        .then_inc(v_Kt.sem, 1)
                meanwhile("kT")
                dve.wait_ge(a_diag.sem, a_diag.at(i, 4))
                dve.wait_ge(p_blk.sem, p_blk.at(i, 2))
                v.transpose(Eb[:], Dg[:]).then_inc(v_blk.sem, 1)
                for r in range(SB - 1):
                    n, w = SB - 1 - r, min(r + 1, SPLIT)
                    dve.wait_ge(v_blk.sem, v_blk.at(i, 1 + 2 * r))
                    tmp_ = tmpb[:, 0:n * w].rearrange("p (a b) -> p a b", a=n)
                    v.tensor_tensor(tmp_, Eb[:, r + 1:, r:r + 1].to_broadcast([P, n, w]),
                                    X[:, r:r + 1, 0:w].to_broadcast([P, n, w]), ALU.mult).then_inc(v_blk.sem, 1)
                    dve.wait_ge(v_blk.sem, v_blk.at(i, 2 + 2 * r))
                    v.tensor_tensor(X[:, r + 1:, 0:w], X[:, r + 1:, 0:w], tmp_, ALU.subtract).then_inc(v_blk.sem, 1)
                    meanwhile(("block", r))
                dve.wait_ge(v_blk.sem, v_blk.at(i, 1 + 2 * (SB - 1)))
                dve.wait_ge(p_blk.sem, p_blk.at(i, p_blk.per))
                v.transpose(XB[:], X[:].rearrange("p t c -> p c t")).then_inc(v_blk.sem, 1)
                for q in (1, 3, 0, 2):
                    off = SB * (q % 2)
                    v.transpose(Z[ROWS[q], :, off:off + SB].rearrange("p u t -> p t u"), X[ROWS[q]])\
                        .then_inc(v_blk.sem, 1)
                low = slice(DH, P)
                for t in range(NT):
                    meanwhile("join" if t == 0 else ("o", 0))
                    if t:
                        with_state(i, 0)
                    meanwhile(("top", t))
                    right = V[:, 0] if t == 0 else R[:]
                    for half in range(2):
                        dve.wait_ge(*full_at(i, ("cross", t, half)))
                        ps = bank(("cross", t, half))
                        if t:
                            dve.wait_ge(p_R1.sem, p_R1.at(i, 2))
                        v.tensor_tensor(R[low, HALF[half], :], right[low, HALF[half], :], by_head(ps)[low],
                                        ALU.subtract).then_inc(v_R.sem, 1)
                    if t:
                        with_state(i, 1)
                        mean_square(i, 0)
                    meanwhile(("cross", t))
                    meanwhile(("low", t))
                    if t == 0:
                        for half in range(2):
                            dve.wait_ge(*full_at(i, ("KS", half)))
                            ps = bank(("KS", half))
                            v.tensor_tensor(R[:, PARITY[half], :], by_head(ps), bc(Gc[:, 0, PARITY[half]], DH), ALU.mult)\
                                .then_inc(v_R.sem, 1)
                        meanwhile("S")
                    for half in range(2):
                        dve.wait_ge(*full_at(i, ("o", t, half)))
                        ps = bank(("o", t, half))
                        dve.wait_ge(p_Dv.sem, p_Dv.at(i, 1 if t == 0 else 4))
                        v.tensor_tensor(O[t][:, HALF[half], :], by_head(ps), Dv[:, HALF[half], :], ALU.add)\
                            .then_inc(v_O.sem, 1)
                    meanwhile(("o", t))
                normalise_x((i, -1))
                mean_square(i, 1)
                meanwhile(None)

            def ffn(j, step, n):
                if step == "y":
                    dve.wait_ge(a_g.sem, a_g.at(j, 4))
                    for t in range(NT):
                        dve.wait_ge(a_sg.sem, a_sg.at(j, t + 1))
                        v.tensor_tensor(O[t], V[:, t], O[t], ALU.mult).then_inc(v_y.sem, 1)
                elif step == "Wo":
                    dve.wait_ge(*full_at(j, "Wo"))
                    dve.wait_ge(p_x1.sem, p_x1.at(j, 1))
                    v.tensor_tensor(x1[:].rearrange("p t d -> p (t d)"), bank("Wo")[:, 0:T],
                                    x1[:].rearrange("p t d -> p (t d)"), ALU.add).then_inc(x1_ready.sem, 1)
                elif step == "ln":
                    dve.wait_ge(x1_ready.sem, x1_ready.at(j, 1))
                    layer_norm(j, x1, fstats, fmv, frstd, xf, f_ln, 0, fp_rstd, 1)
                    dve.wait_ge(f_ln.sem, f_ln.at(j, 5))
                    layer_norm(j, xf, fstats, fmv, frstd, hn, f_ln, 5, fp_rstd, 2)
                elif step == "fqk":
                    dve.wait_ge(*full_at(j, "fqk"))
                    ps = pair(bank("fqk"))
                    v.tensor_copy(part[:, 0], ps).then_inc(v_part.sem, 1)
                    dve.wait_ge(v_part.sem, v_part.at(j, 1))
                    v.tensor_tensor(prest[:], ps, part[:, 0], ALU.subtract).then_inc(v_part.sem, 1)
                    dve.wait_ge(v_part.sem, v_part.at(j, 2))
                    v.tensor_copy(part[:, 1], prest[:]).then_inc(v_part.sem, 1)
                    dve.wait_ge(v_part.sem, v_part.at(j, 3))
                    v.tensor_tensor(part[:, 2], prest[:], part[:, 1], ALU.subtract).then_inc(v_part.sem, 1)
                elif step == "fv":
                    dve.wait_ge(*full_at(j, "fv"))
                    ps = bank("fv")
                    v.tensor_copy(v9_tile()[:, :, :, 0:FD], ps[:, 0:T].rearrange("p (t h d) -> p t h d", t=NT, h=FH))\
                        .then_inc(v_v9.sem, 1)
                elif step == "max":
                    dve.wait_ge(*full_at(j, ("max", n)))
                    ps = pair(bank(("max", n)))
                    v.tensor_reduce(mx[:, :, n], ps, AX.X, ALU.max).then_inc(v_mx.sem, 1)
                elif step == "mrow" and n == 0:
                    dve.wait_ge(v_mx.sem, v_mx.at(j, FH))
                    v.tensor_scalar(mpart[:, 0], mx[:], -1.0, None, ALU.mult).then_inc(v_mp.sem, 1)
                    dve.wait_ge(v_mp.sem, v_mp.at(j, 1))
                    v.scalar_tensor_tensor(mrest[:], mx[:], -1.0, mpart[:, 0], ALU.mult, ALU.subtract)\
                        .then_inc(v_mp.sem, 1)
                    dve.wait_ge(v_mp.sem, v_mp.at(j, 2))
                    v.tensor_copy(mpart[:, 1], mrest[:]).then_inc(v_mp.sem, 1)
                    dve.wait_ge(v_mp.sem, v_mp.at(j, 3))
                    v.tensor_tensor(mpart[:, 2], mrest[:], mpart[:, 1], ALU.subtract).then_inc(v_mp.sem, 1)
                    dve.wait_ge(v_mp.sem, v_mp.at(j, 4))
                    v.tensor_copy(mpad[:, :, :, ROW6:ROW6 + NS], mpart[:].rearrange("p s t h -> p t h s"))\
                        .then_inc(v_mp.sem, 1)
                if step == "mrow":
                    dve.wait_ge(*full_at(j, ("mrow", n)))
                    ps = pair(bank(("mrow", n)))
                    v.tensor_tensor(QK6[:, 2 * n:2 * n + 2, 0, :], QK6[:, 2 * n:2 * n + 2, 0, :], ps, ALU.add)\
                        .then_inc(v_mrow.sem, 1)
                elif step == "ctx":
                    dve.wait_ge(*full_at(j, ("ctx", n)))
                    ps = bank(("ctx", n))[:].rearrange("p (h d) -> p h d", h=FH)
                    v.reciprocal(rec[:, n, :], ps[:, :, FD]).then_inc(v_ctx.sem, 1)
                    dve.wait_ge(v_ctx.sem, v_ctx.at(j, 2 * n + 1))
                    v.tensor_tensor(ctxn[:, n, :].rearrange("p (h d) -> p h d", h=FH), ps[:, :, 0:FD],
                                    bc(rec[:, n, :], FD), ALU.mult).then_inc(v_ctx.sem, 1)
                elif step == "fWo":
                    dve.wait_ge(*full_at(j, "fWo"))
                    ps = bank("fWo")
                    v.tensor_tensor(x2[:].rearrange("p t d -> p (t d)"), ps[:, 0:T], xf[:].rearrange("p t d -> p (t d)"),
                                    ALU.add).then_inc(v_x2.sem, 1)
                    dve.wait_ge(v_x2.sem, v_x2.at(j, 1))
                    layer_norm(j, x2, fstats, fmv, frstd, hn, f_ln, 10, fp_rstd, 3)
                elif step == "router":
                    dve.wait_ge(*full_at(j, "router"))
                    ps = bank("router")
                    l_ = ps[:, 0:NT * NE].rearrange("p (t e) -> p t e", t=NT)
                    v.tensor_reduce(lmax[:], l_, AX.X, ALU.max).then_inc(v_lg.sem, 1)
                    dve.wait_ge(v_lg.sem, v_lg.at(j, 1))
                    v.tensor_tensor(lg[:], l_, bc(lmax[:], NE), ALU.subtract).then_inc(v_lg.sem, 1)
                    dve.wait_ge(a_ex.sem, a_ex.at(j, 1))
                    mine = ex[:].unsqueeze(3).to_broadcast([P, NT, NE, NE])
                    other = ex[:].unsqueeze(2).to_broadcast([P, NT, NE, NE])
                    v.tensor_tensor(gt[:], other, mine, ALU.is_gt).then_inc(v_w.sem, 1)
                    v.tensor_tensor(eq[:], other, mine, ALU.is_equal).then_inc(v_w.sem, 1)
                    dve.wait_ge(v_w.sem, v_w.at(j, 2))
                    v.tensor_tensor(eq[:], eq[:], earlier[:].rearrange("p (a b) -> p a b", a=NE).unsqueeze(1)
                                    .to_broadcast([P, NT, NE, NE]), ALU.mult).then_inc(v_w.sem, 1)
                    dve.wait_ge(v_w.sem, v_w.at(j, 3))
                    v.tensor_tensor(gt[:], gt[:], eq[:], ALU.add).then_inc(v_w.sem, 1)
                    dve.wait_ge(v_w.sem, v_w.at(j, 4))
                    v.tensor_reduce(rank[:], gt[:], AX.X, ALU.add).then_inc(v_w.sem, 1)
                    dve.wait_ge(v_w.sem, v_w.at(j, 5))
                    v.scalar_tensor_tensor(wsel[:], rank[:], 2.0, ex[:], ALU.is_lt, ALU.mult).then_inc(v_w.sem, 1)
                    dve.wait_ge(v_w.sem, v_w.at(j, 6))
                    v.tensor_reduce(wden[:], wsel[:], AX.X, ALU.add).then_inc(v_w.sem, 1)
                    dve.wait_ge(v_w.sem, v_w.at(j, 7))
                    v.reciprocal(wden[:], wden[:]).then_inc(v_w.sem, 1)
                    dve.wait_ge(v_w.sem, v_w.at(j, 8))
                    v.tensor_tensor(wsel[:], wsel[:], bc(wden[:], NE), ALU.mult).then_inc(v_w.sem, 1)
                elif step == "wT":
                    dve.wait_ge(*full_at(j, "wT"))
                    ps = bank("wT")
                    v.tensor_copy(wT[:], ps[0:NE, 0:T]).then_inc(v_wT.sem, 1)
                elif step == "b2":
                    dve.wait_ge(*full_at(j, "b2"))
                    ps = bank("b2")
                    dve.wait_ge(p_xs.sem, p_xs.at(j, 1))
                    if not (isinstance(j, int) and j == 0):
                        dve.wait_ge(out_stored.sem, out_stored.at(j, 0))
                    v.tensor_tensor(moe[:].rearrange("p t d -> p (t d)"), ps[:, 0:T], x1[:].rearrange("p t d -> p (t d)"),
                                    ALU.add).then_inc(v_moe.sem, 1)
                elif step == "down":
                    dve.wait_ge(*full_at(j, ("y", n)))
                    ps = bank(("y", n))
                    dve.wait_ge(v_moe.sem, v_moe.at(j, n + 1))
                    for t in range(NT):
                        ins = v.scalar_tensor_tensor(moe[:, t, :], ps[:, TOK[t]], wsel[:, t, n:n + 1], moe[:, t, :],
                                                     ALU.mult, ALU.add)
                    ins.then_inc(v_moe.sem, 1)

            batches(dve, gdn, ffn, lambda: normalise_x(0))



def tables():
    c = {"c_ident": np.eye(P)}
    pad = np.zeros((P, NT, GW))
    pad[:, :, 1:] = np.eye(P)[:, None, :]
    c["c_ident_pad"] = pad.reshape(P, -1)
    inv = (1.0 / np.float32(10000.0) ** (np.arange(0, DH, 2, dtype=np.float32) / np.float32(DH))).astype(np.float32)
    freqs = np.outer(np.arange(T, dtype=np.float32), inv).astype(np.float32)
    emb = np.concatenate([freqs, freqs], -1)[:, ::2]
    rows = np.arange(P) % DH // 2
    sign = np.where(np.arange(P) % 2 == 0, -1.0, 1.0)[:, None]
    c["c_cos"] = np.cos(emb)[:, rows].T
    c["c_sin"] = np.sin(emb)[:, rows].T * sign
    c["c_head_cols"] = (np.arange(P)[:, None] // DH + H - 2 == np.arange(2 * (H - 1) + 16)[None, :])
    sel = np.zeros((P, H, P))
    for h in range(H):
        sel[[h, 32 + h, 64 + h], h, :] = 1.0
    c["c_alpha_sel"] = sel.reshape(P, -1)
    for name, split in (("c_q_sel", SPLIT_Q), ("c_k_sel", SPLIT_K)):
        sel = np.zeros((P, NS, NC, P))
        for h in range(FH):
            for n, s in enumerate(split):
                for d in range(FD):
                    sel[h * FD + d, s, h // 2, (h % 2) * DH + n * FD + d] = 1.0
        c[name] = sel.reshape(P, -1)
    r = np.arange(P) % DH
    c["c_k_ones"] = ((r >= ROW6) & (r < ROW6 + NS))[:, None]
    c["c_earlier"] = np.tile((np.arange(NE)[None, :] < np.arange(NE)[:, None]).reshape(1, -1), (P, 1))
    return {k: np.ascontiguousarray(x, dtype=np.float32) for k, x in c.items()}


def kernel(**inputs):
    import concourse.bacc as bacc
    from concourse.bass_utils import run_bass_kernel_spmd

    x = {k: np.asarray(a) for k, a in inputs.items()}
    att = {k[len("L0_attn_"):]: a for k, a in x.items() if k.startswith("L0_attn_")}
    ffn = {k[len("L0_ffn_"):]: a for k, a in x.items() if k.startswith("L0_ffn_")}
    arrays = {k: att[k] for k in ("x", "Wq", "Wk", "Wv", "Wg", "Wo", "bw", "bb", "gkw", "gkb", "dt_bias", "A_log",
                                  "D_param", "onorm_w")}
    arrays["conv_w"] = np.stack([att[k][:, 0, :].reshape(NC, P, KT).transpose(1, 0, 2) for k in ("qcw", "kcw", "vcw")], 1)
    arrays["conv_b"] = np.stack([att[k].reshape(NC, P).T for k in ("qcb", "kcb", "vcb")], 1)
    for k in ("Wq", "Wk", "Wv", "Wo", "Wg"):
        arrays["f" + k] = ffn[k]
    for k in ("ln1_g", "ln1_b", "ln2_g", "ln2_b"):
        arrays[k] = ffn[k].reshape(HID, 1)
    arrays["W1"], arrays["W2"], arrays["b2"] = ffn["W1"], ffn["W2"], ffn["b2"]
    arrays["b1"] = ffn["b1"].reshape(NE, NF, P).transpose(2, 0, 1)
    arrays.update(tables())

    nc = bacc.Bacc("TRN2", target_bir_lowering=False, num_devices=1)
    feed, args = {}, {}
    for k, v in arrays.items():
        v = np.ascontiguousarray(v)
        feed[f"in_{k}"] = v
        args[k] = nc.dram_tensor(f"in_{k}", v.shape, mybir.dt.from_np(v.dtype), kind="ExternalInput").ap()
    out = nc.dram_tensor("out", x["L0_attn_x"].shape, F32, kind="ExternalOutput").ap()
    program(nc, args, out)
    r = run_bass_kernel_spmd(nc, [feed], core_ids=[0])
    return r.results[0]["out"]
```
